# Optimizing a Trainium2 kernel written in Bass

```python
import numpy as np
import jax
import jax.numpy as jnp

def _softmax(x, axis=-1):
    return jax.nn.softmax(x, axis=axis)

def _gelu(x):
    return jax.nn.gelu(x, approximate=True)

def _silu(x):
    return jax.nn.silu(x)

def _sigmoid(x):
    return jax.nn.sigmoid(x)

def _layernorm(x, axis=-1, eps=1e-05):
    m = jnp.mean(x, axis=axis, keepdims=True)
    v = jnp.var(x, axis=axis, keepdims=True)
    return (x - m) / jnp.sqrt(v + eps)

def _scatter_add(tgt, idx, src, axis=0):
    return tgt.at[idx].add(src)

def _segment_sum(src, seg, n):
    return jax.ops.segment_sum(src, seg, n)
kernel_name = 'mk_gnn_resnorm_d2_gnn_r8_2eb014'

def setup_inputs(seed: int=0):
    np.random.seed(seed)
    _w = jnp.asarray

    def _rec_inputs():
        import jax
        import jax.numpy as jnp
        _gk = jax.random.key(seed)
        x = -0.000202 + 1 * jax.random.normal(jax.random.fold_in(_gk, 1), (6250, 128), jnp.float32)
        _s = jax.random.randint(jax.random.fold_in(_gk, 2), (50000,), 0, 6250, jnp.int32)
        _d = jax.random.randint(jax.random.fold_in(_gk, 3), (50000,), 0, 6250, jnp.int32)
        _loop = jnp.arange(6250, dtype=jnp.int32)
        src = jnp.concatenate([_s, _d, _loop])
        dst = jnp.concatenate([_d, _s, _loop])
        _o = jnp.argsort(dst, stable=True)
        src = src[_o]
        dst = dst[_o]
        edge_attr_128 = -8.16379e-05 + 0.999858 * jax.random.normal(jax.random.fold_in(_gk, 12), (106250, 128), jnp.float32)
        return (x, src, dst, edge_attr_128)
    x, src, dst, edge_attr_128 = _rec_inputs()

    def _L0_gnn_setup():
        import jax, jax.numpy as jnp
        import numpy as np
        N_NODES = 6250
        N_EDGES = 100000
        D = 128
        key = jax.random.key(seed)
        ks = jax.random.split(key, 8)
        nfeats = jax.random.normal(ks[0], (N_NODES, D), dtype=jnp.float32)
        efeats = jax.random.normal(ks[1], (N_EDGES, D), dtype=jnp.float32)
        src = jax.random.randint(ks[2], (N_EDGES,), 0, N_NODES, dtype=jnp.int32)
        dst = jax.random.randint(ks[3], (N_EDGES,), 0, N_NODES, dtype=jnp.int32)
        W_msg_w = jax.random.normal(ks[4], (D, 2 * D), dtype=jnp.float32) * (1.0 / np.sqrt(2 * D))
        W_msg_b = jnp.zeros((D,), dtype=jnp.float32)
        W_app_w = jax.random.normal(ks[5], (D, 2 * D), dtype=jnp.float32) * (1.0 / np.sqrt(2 * D))
        W_app_b = jnp.zeros((D,), dtype=jnp.float32)
        return {'nfeats': nfeats, 'efeats': efeats, 'src': src, 'dst': dst, 'W_msg_w': W_msg_w, 'W_msg_b': W_msg_b, 'W_app_w': W_app_w, 'W_app_b': W_app_b}
    _L0_gnn_all = _L0_gnn_setup()
    _L0_gnn_in = {k: v for k, v in _L0_gnn_all.items() if k in ('W_msg_w', 'W_msg_b', 'W_app_w', 'W_app_b')}
    del _L0_gnn_all

    def _L1_gnn_setup():
        import jax, jax.numpy as jnp
        import numpy as np
        N_NODES = 6250
        N_EDGES = 100000
        H = 128
        LN_EPS = 1e-05
        key = jax.random.key(seed)
        ks = jax.random.split(key, 8)
        x = jax.random.normal(ks[0], (N_NODES, H), dtype=jnp.float32)
        edge_index = jax.random.randint(ks[1], (2, N_EDGES), 0, N_NODES, dtype=jnp.int64)
        W1 = jax.random.normal(ks[2], (2 * H, H), dtype=jnp.float32) * 0.02
        b1 = jnp.zeros((H,), dtype=jnp.float32)
        W2 = jax.random.normal(ks[3], (H, 1), dtype=jnp.float32) * 0.02
        b2 = jnp.zeros((1,), dtype=jnp.float32)
        gamma = jnp.ones((H,), dtype=jnp.float32)
        beta = jnp.zeros((H,), dtype=jnp.float32)
        return {'x': x, 'edge_index': edge_index, 'W1': W1, 'b1': b1, 'W2': W2, 'b2': b2, 'gamma': gamma, 'beta': beta}
    _L1_gnn_all = _L1_gnn_setup()
    _L1_gnn_in = {k: v for k, v in _L1_gnn_all.items() if k in ('W1', 'b1', 'W2', 'b2', 'gamma', 'beta')}
    del _L1_gnn_all
    return {'x': x, 'src': src, 'dst': dst, 'edge_attr_128': edge_attr_128, 'L0_gnn_W_msg_w': _L0_gnn_in['W_msg_w'], 'L0_gnn_W_msg_b': _L0_gnn_in['W_msg_b'], 'L0_gnn_W_app_w': _L0_gnn_in['W_app_w'], 'L0_gnn_W_app_b': _L0_gnn_in['W_app_b'], 'L1_gnn_W1': _L1_gnn_in['W1'], 'L1_gnn_b1': _L1_gnn_in['b1'], 'L1_gnn_W2': _L1_gnn_in['W2'], 'L1_gnn_b2': _L1_gnn_in['b2'], 'L1_gnn_gamma': _L1_gnn_in['gamma'], 'L1_gnn_beta': _L1_gnn_in['beta']}

def reference(x, src, dst, edge_attr_128, L0_gnn_W_msg_w, L0_gnn_W_msg_b, L0_gnn_W_app_w, L0_gnn_W_app_b, L1_gnn_W1, L1_gnn_b1, L1_gnn_W2, L1_gnn_b2, L1_gnn_gamma, L1_gnn_beta):
    import jax
    import jax.numpy as jnp

    def _L0_gnn_ref(nfeats, efeats, src, dst, W_msg_w, W_msg_b, W_app_w, W_app_b):
        import jax, jax.numpy as jnp
        import numpy as np
        N_NODES = 6250
        N_EDGES = 100000
        D = 128
        msg_in = jnp.concatenate([nfeats[src], efeats], axis=-1)
        msg = msg_in @ W_msg_w.T + W_msg_b
        msg_sum = jax.ops.segment_sum(msg, dst, num_segments=N_NODES)
        deg = jax.ops.segment_sum(jnp.ones((msg.shape[0],), msg.dtype), dst, num_segments=N_NODES)
        h_neigh = jnp.where(deg[:, None] > 0, msg_sum / jnp.maximum(deg, 1.0)[:, None], jnp.zeros_like(msg_sum))
        apply_in = jnp.concatenate([nfeats, h_neigh], axis=-1)
        return jax.nn.relu(apply_in @ W_app_w.T + W_app_b)

    def _L1_gnn_ref(x, edge_index, W1, b1, W2, b2, gamma, beta):
        import jax, jax.numpy as jnp
        import numpy as np
        N_NODES = 6250
        N_EDGES = 100000
        H = 128
        LN_EPS = 1e-05
        src = edge_index[0]
        tgt = edge_index[1]
        edge_feat = jnp.concatenate([x[src], x[tgt]], axis=1)
        h = jax.nn.relu(edge_feat @ W1 + b1)
        w = jax.nn.sigmoid(h @ W2 + b2)[:, 0]
        agg = jax.ops.segment_sum(w[:, None] * x[src], tgt, num_segments=x.shape[0])
        attended = x + agg
        mu = jnp.mean(attended, axis=-1, keepdims=True)
        var = jnp.mean(jnp.square(attended - mu), axis=-1, keepdims=True)
        out = (attended - mu) * jax.lax.rsqrt(var + LN_EPS) * gamma + beta
        return out
    edge_index = jnp.stack([src, dst])
    x = _layernorm(x + _L0_gnn_ref(x, edge_attr_128, src, dst, L0_gnn_W_msg_w, L0_gnn_W_msg_b, L0_gnn_W_app_w, L0_gnn_W_app_b), axis=-1)
    x = _layernorm(x + _L1_gnn_ref(x, edge_index, L1_gnn_W1, L1_gnn_b1, L1_gnn_W2, L1_gnn_b2, L1_gnn_gamma, L1_gnn_beta), axis=-1)
    return x

_drawn_inputs = setup_inputs


def setup_inputs(seed=0):
    import zlib

    import numpy as np

    out = dict(_drawn_inputs(seed))
    spreads = {'L0_gnn_W_msg_b': (0.0, 0.1),
     'L0_gnn_W_app_b': (0.0, 0.1),
     'L1_gnn_b1': (0.0, 0.8),
     'L1_gnn_gamma': (1.0, 0.2),
     'L1_gnn_beta': (0.0, 0.1)}
    factors = {'L1_gnn_W1': 6.928, 'L1_gnn_W2': 6.693}
    for name, (base, spread) in spreads.items():
        noise = np.random.default_rng([zlib.crc32(name.encode()), seed]).standard_normal(out[name].shape)
        drawn = base * np.exp(spread * noise) if base else spread * noise
        out[name] = jnp.asarray(drawn.astype(out[name].dtype))
    for name, factor in factors.items():
        out[name] = (out[name] * factor).astype(out[name].dtype)
    return out
```

```python
import concourse.bass as bass
from concourse import mybir
from contextlib import ExitStack

F32 = mybir.dt.float32
BF16 = mybir.dt.bfloat16
I32 = mybir.dt.int32
ALU = mybir.AluOpType
ACT = mybir.ActivationFunctionType
AX_X = mybir.AxisListType.X

E, N, D = 106250, 6250, 128
P = 128
TILES = 8
GE = P * TILES
G = -(-E // GE)
FULL = E // GE
REST = E - FULL * GE
REST_P, REST_J = REST // TILES, REST % TILES
SLOTS = 4
TURNS = G // SLOTS
W = 128
NB = G // 2
BN = -(-N // NB)
NPAD = NB * BN
LAST_BN = N - (NB - 1) * BN
BASE_MAX = NPAD - W
EPS = 1e-5
NO_NODE = 30000
DMA = 16
LAG0 = 4
LN0_STEPS, LN1_STEPS = 6, 10
WINDOWS = -(-NPAD // W)


def back(i, u, d):
    return i + (u - d) // SLOTS, (u - d) % SLOTS


def ahead(i, u):
    return i + (u + 1) // SLOTS, (u + 1) % SLOTS


def there(i):
    return not isinstance(i, int) or i >= 0


def is_last(i, u):
    return isinstance(i, int) and SLOTS * i + u == G - 1


def build(nc, x, src, dst, edge, w_msg, b_msg, w_app, b_app, w1, b1, w2, b2, gamma, beta, out):
    ctx = ExitStack()

    def sb(name, shape, dt=F32):
        return ctx.enter_context(nc.sbuf_tensor(name, shape, dt))

    def sem(name):
        return ctx.enter_context(nc.semaphore(name))

    def sems(name, n):
        return [sem(f"{name}{k}") for k in range(n)]

    with ctx:
        table = nc.dram_tensor("table", (NPAD, 2 * D), F32, kind="Internal").ap()
        q_parts = nc.dram_tensor("q_parts", (NPAD, 3 * D), BF16, kind="Internal").ap()
        rel_rows = nc.dram_tensor("rel_rows", (G, GE), BF16, kind="Internal").ap()

        src_g = src[0:FULL * GE].rearrange("(g p j) -> g p j", p=P, j=TILES)
        dst_g = dst[0:FULL * GE].rearrange("(g p j) -> g p j", p=P, j=TILES)
        edge_g = edge[0:FULL * GE, :].rearrange("(g p j) d -> g p (j d)", p=P, j=TILES)
        src_rest, dst_rest = (a[FULL * GE:FULL * GE + REST_P * TILES].rearrange("(p j) -> p j", j=TILES)
                              for a in (src, dst))
        edge_rest = edge[FULL * GE:FULL * GE + REST_P * TILES, :].rearrange("(p j) d -> p (j d)", j=TILES)
        src_end, dst_end = (a[E - REST_J:E].rearrange("(p j) -> p j", p=1) for a in (src, dst))
        edge_end = edge[E - REST_J:E, :].rearrange("(p j) d -> p (j d)", p=1)

        ident = sb("ident", [P, P])
        identb = sb("identb", [P, P], BF16)
        ones = sb("ones", [P, P])
        iota_w = sb("iota_w", [P, W])
        iota_i = sb("iota_i", [P, W], I32)
        iota_pi = sb("iota_pi", [P, 1], I32)
        iota_p = sb("iota_p", [P, 1])
        wmsg_sb = sb("wmsg_sb", [D, 2 * D])
        wapp_sb = sb("wapp_sb", [D, 2 * D])
        wT = sb("wT", [D, 4, D])
        w1_sb = sb("w1_sb", [D, 2 * D])
        rows = sb("rows", [1, 6 * D])
        b2_row = sb("b2_row", [1, 1])
        bcast = sb("bcast", [P, 3, D])
        b2_neg = sb("b2_neg", [P, 1])
        dst_nat = sb("dst_nat", [G, GE], I32)
        dst_f = sb("dst_f", [G, GE])
        rel_nat = sb("rel_nat", [G, GE], BF16)
        low = sb("low", [G, 1])
        high = sb("high", [G, 1])
        base = sb("base", [G, 1])
        floor_i = sb("floor_i", [G, 1], I32)
        floor = sb("floor", [G, 1])
        spread = sb("spread", [G, 1])
        fits = sb("fits", [G, 2])
        ok = sb("ok", [G, 1])
        base_l = sb("base_l", [G, P])
        base_bc = sb("base_bc", [P, G])
        base_i = sb("base_i", [1, G], I32)
        ok_i = sb("ok_i", [1, 1], I32)
        no_node = sb("no_node", [P, TILES], I32)

        src_slot = sb("src_slot", [P, SLOTS, TILES], I32)
        dst_slot = sb("dst_slot", [P, SLOTS, TILES], I32)
        rel = sb("rel", [P, G * TILES])
        ring = sb("ring", [P, SLOTS, 2 * GE])
        S = sb("S", [P, SLOTS, TILES, W])
        S_sum = sb("S_sum", [P, SLOTS, W])
        acc_x = sb("acc_x", [D, WINDOWS * W])
        acc_e = sb("acc_e", [D, WINDOWS * W])
        acc_deg = sb("acc_deg", [1, WINDOWS * W])
        x_blk = sb("x_blk", [BN, 2, D])
        n_x = sb("n_x", [D, 2, BN])
        n_e = sb("n_e", [D, 2, BN])
        n_deg = sb("n_deg", [1, 2, BN])
        hsT = sb("hsT", [D, 2, BN])
        xT = sb("xT", [D, 2, BN])
        x1T = sb("x1T", [D, 2, BN])
        deg_max = sb("deg_max", [BN, 2])
        deg_inv = sb("deg_inv", [BN, 2])
        z = sb("z", [BN, 2, D])
        y = sb("y", [BN, 2, D])
        stats = sb("stats", [BN, 2, 6])
        moments = sb("moments", [BN, 2, 2])
        log_var = sb("log_var", [BN, 2])
        rstd = sb("rstd", [BN, 2])
        eps_col = sb("eps_col", [BN, 1])
        tab_blk = sb("tab_blk", [BN, 2, 2 * D])
        q_blk = sb("q_blk", [BN, 2, 3 * D], BF16)
        q_rest = sb("q_rest", [BN, 2, 2, D])
        rel_bc = sb("rel_bc", [P, SLOTS, GE], BF16)
        ST = sb("ST", [P, SLOTS, TILES, P], BF16)
        q_win = sb("q_win", [P, SLOTS, 3 * D], BF16)
        act_out = sb("act_out", [P, TILES, D])
        logit = sb("logit", [P, SLOTS, TILES])
        expm = sb("expm", [P, SLOTS, TILES])
        expm1 = sb("expm1", [P, SLOTS, TILES])
        weight = sb("weight", [P, SLOTS, TILES])
        fin = sb("fin", [BN, 2, D])
        q_rows = ST[:, :, :, :].rearrange("p s t c -> p (s t c)")[:, 0:3 * GE]

        def bank(name):
            return ctx.enter_context(nc.psum_tensor(name, [P, 512], F32))

        ps_agg = [bank("ps_agg0"), bank("ps_agg1")]
        ps4 = [bank(f"ps4_{k}") for k in range(4)]
        ps_fin = [bank("ps_fin0"), bank("ps_fin1")]

        ld_dst, ld_par, memset_ok, iota_ok = sem("ld_dst"), sem("ld_par"), sem("memset_ok"), sem("iota_ok")
        ident_ok, dve_pro, pe_pro, act_pro = sem("ident_ok"), sem("dve_pro"), sem("pe_pro"), sem("act_pro")
        rel_out = sem("rel_out")
        src_in0, dst_in, edge_in, gath0 = sems("src_in0_", 4), sems("dst_in", 4), sems("edge_in", 4), sems("gath0_", 4)
        pad_in = sem("pad_in")
        rel_done, s_ready, sum_ready, agg0, acc0 = (sem(n) for n in ("rel_done", "s_ready", "sum_ready", "agg0", "acc0"))
        x_in = sems("x_in", 2)
        cut, prod, prod_cp, deg_steps, mix, ln0 = (sem(n) for n in ("cut", "prod", "prod_cp", "deg_steps", "mix", "ln0"))
        x1_tr, x1_cp, pq, p_cp, q_steps = (sem(n) for n in ("x1_tr", "x1_cp", "pq", "p_cp", "q_steps"))
        q_split, log_done, rstd0, rstd1 = sem("q_split"), sem("log_done"), sem("rstd0"), sem("rstd1")
        tab_out = sems("tab_out", 2)
        cleared = sem("cleared")
        src_in1, gath1, row_in, q_in = sems("src_in1_", 4), sems("gath1_", 4), sems("row_in", 4), sems("q_in", 4)
        st_ready, h_done, dot_done, sig_done, sw_ready, agg1, acc1 = (
            sem(n) for n in ("st_ready", "h_done", "dot_done", "sig_done", "sw_ready", "agg1", "acc1"))
        x1_in, cut1, sum_tr, ln1 = sems("x1_in", 2), sem("cut1"), sem("sum_tr"), sem("ln1")
        w_steps = sem("w_steps")
        fin_out, passed = sems("fin_out", 2), sem("passed")

        pro = nc.Block()
        with pro as block:
            @block.sync
            def _(sp):
                sp.wait_ge(memset_ok, 1)
                sp.dma_start(dst_nat[0:FULL, :], dst[0:FULL * GE].rearrange("(g e) -> g e", e=GE)).then_inc(ld_dst, DMA)
                sp.dma_start(dst_nat[FULL:G, 0:REST], dst[FULL * GE:E].rearrange("(g e) -> g e", g=1)).then_inc(ld_dst, DMA)
                sp.dma_start(wmsg_sb[:, :], w_msg).then_inc(ld_par, DMA)
                sp.dma_start(wapp_sb[:, :], w_app).then_inc(ld_par, DMA)
                for k in range(2):
                    sp.dma_start(w1_sb[:, k * D:(k + 1) * D], w1[k * D:(k + 1) * D, :]).then_inc(ld_par, DMA)
                for k, v in enumerate((b_msg, b_app, b1, w2.rearrange("f o -> (f o)"), gamma, beta)):
                    sp.dma_start(rows[0:1, k * D:(k + 1) * D], v.rearrange("(o f) -> o f", o=1)).then_inc(ld_par, DMA)
                sp.dma_start(b2_row[:, :], b2.rearrange("(o f) -> o f", o=1)).then_inc(ld_par, DMA)
                sp.wait_ge(dve_pro, 4)
                sp.dma_start(rel_rows, rel_nat[:, :]).then_inc(rel_out, DMA)
                sp.wait_ge(rel_out, DMA)

            @block.gpsimd
            def _(pool):
                nc.gpsimd.iota(iota_i[:, :], pattern=[[1, W]], base=0, channel_multiplier=0).then_inc(iota_ok, 1)
                nc.gpsimd.iota(iota_pi[:, :], pattern=[[0, 1]], base=0, channel_multiplier=1).then_inc(iota_ok, 1)
                nc.gpsimd.memset(ident[:, :], 0.0).then_inc(iota_ok, 1)
                pool.wait_ge(iota_ok, 3)
                nc.gpsimd.affine_select(out=ident[:, :], in_=ident[:, :], compare_op=ALU.not_equal, fill=1.0, base=0,
                                        pattern=[[-1, P]], channel_multiplier=1).then_inc(ident_ok, 1)

            @block.vector
            def _(dve):
                nc.vector.memset(dst_nat[:, :], N - 1).then_inc(memset_ok, 1)
                nc.vector.memset(ones[:, :], 1.0)
                nc.vector.memset(eps_col[:, :], EPS)
                nc.vector.memset(no_node[:, :], NO_NODE)
                nc.vector.memset(acc_x[:, :], 0.0)
                nc.vector.memset(acc_e[:, :], 0.0)
                nc.vector.memset(acc_deg[:, :], 0.0).then_inc(memset_ok, 1)
                dve.wait_ge(iota_ok, 2)
                nc.vector.tensor_copy(iota_w[:, :], iota_i[:, :])
                nc.vector.tensor_copy(iota_p[:, :], iota_pi[:, :])
                nc.vector.tensor_scalar(floor_i[:, :], iota_pi[0:G, :], 1, None, ALU.arith_shift_right).then_inc(memset_ok, 1)
                dve.wait_ge(memset_ok, 3)
                nc.vector.tensor_scalar(floor[:, :], floor_i[:, :], float(BN), float(-BN), ALU.mult, ALU.add)
                dve.wait_ge(ld_dst, 2 * DMA)
                nc.vector.tensor_copy(dst_f[:, :], dst_nat[:, :]).then_inc(dve_pro, 1)
                dve.wait_ge(dve_pro, 1)
                nc.vector.tensor_reduce(low[:, :], dst_f[:, :], AX_X, ALU.min)
                nc.vector.tensor_reduce(high[:, :], dst_f[:, :], AX_X, ALU.max).then_inc(dve_pro, 1)
                dve.wait_ge(dve_pro, 2)
                nc.vector.tensor_scalar(base[:, :], low[:, :], float(BASE_MAX), None, ALU.min).then_inc(dve_pro, 1)
                dve.wait_ge(dve_pro, 3)
                nc.vector.tensor_scalar(rel_nat[:, :], dst_f[:, :], base[:, 0:1], None, ALU.subtract).then_inc(dve_pro, 1)
                nc.vector.tensor_scalar(base_l[:, :], ones[0:G, :], base[:, 0:1], None, ALU.mult)
                nc.vector.tensor_tensor(spread[:, :], high[:, :], base[:, :], ALU.subtract)
                nc.vector.tensor_tensor(fits[:, 1:2], low[:, :], floor[:, :], ALU.is_ge).then_inc(dve_pro, 1)
                dve.wait_ge(dve_pro, 5)
                nc.vector.tensor_scalar(fits[:, 0:1], spread[:, :], float(W - 1), None, ALU.is_le).then_inc(dve_pro, 1)
                dve.wait_ge(dve_pro, 6)
                nc.vector.tensor_tensor(ok[:, :], fits[:, 0:1], fits[:, 1:2], ALU.mult).then_inc(dve_pro, 1)
                dve.wait_ge(ident_ok, 1)
                nc.vector.tensor_copy(identb[:, :], ident[:, :])
                dve.wait_ge(pe_pro, 2)
                nc.vector.tensor_copy(base_bc[:, :], ps_agg[0][:, 0:G])
                nc.vector.tensor_copy(base_i[:, :], ps_agg[0][0:1, 0:G])
                nc.vector.tensor_copy(ok_i[:, :], ps_agg[1][0:1, 0:1])

            @block.tensor
            def _(pe):
                pe.wait_ge(ident_ok, 1)
                pe.wait_ge(memset_ok, 2)
                pe.wait_ge(ld_par, 11 * DMA)
                for k, w in enumerate((wmsg_sb, wmsg_sb, wapp_sb, wapp_sb)):
                    nc.tensor.transpose(ps4[0][:, k * D:(k + 1) * D], w[:, (k % 2) * D:(k % 2 + 1) * D], ident[:, :])
                nc.tensor.matmul(ps4[1][:, 0:3 * D], ones[0:1, :], rows[0:1, 3 * D:6 * D], start=True, stop=True)
                nc.tensor.matmul(ps4[2][:, 0:1], ones[0:1, :], b2_row[:, :], start=True, stop=True).then_inc(pe_pro, 1)
                pe.wait_ge(dve_pro, 7)
                nc.tensor.matmul(ps_agg[0][:, 0:G], base_l[:, :], ident[0:G, 0:G], start=True, stop=True)
                nc.tensor.matmul(ps_agg[1][0:1, 0:1], ok[:, :], ones[0:G, 0:1], start=True, stop=True).then_inc(pe_pro, 1)

            @block.scalar
            def _(act):
                act.wait_ge(pe_pro, 1)
                nc.scalar.copy(wT[:, :, :].rearrange("p a b -> p (a b)"), ps4[0][:, :])
                nc.scalar.copy(bcast[:, :, :].rearrange("p a b -> p (a b)"), ps4[1][:, 0:3 * D])
                nc.scalar.mul(b2_neg[:, :], ps4[2][:, 0:1], -1.0)

        fitting = nc.values_load(ok_i[0:1, 0:1], min_val=0, max_val=G)

        waT, wbT, wcT, wdT = (wT[:, k, :] for k in range(4))
        b_msg_row, b_app_row, b1_row = (rows[0:1, k * D:(k + 1) * D] for k in range(3))
        w2_bc, gamma_bc, beta_bc = (bcast[0:P, k, :] for k in range(3))

        def wait_apart(eng, semaphore, value):
            eng.wait_ge(semaphore, value)
            eng.sem_inc(passed, 1)

        def norm_steps(dve, done, at, inv_done, inv_at, v, values, result):
            nc.vector.bn_stats(stats[:, v, :], values).then_inc(done, 1)
            wait_apart(dve, done, at + 1)
            nc.vector.bn_aggr(moments[:, v, :], stats[:, v, :]).then_inc(done, 1)
            dve.wait_ge(done, at + 2)
            dve.wait_ge(inv_done, inv_at + 1)
            nc.vector.tensor_scalar(result, values, moments[:, v, 0:1], rstd[:, v:v + 1], ALU.subtract,
                                    ALU.mult).then_inc(done, 1)

        def act_rstd(act, done, at, inv_done, log_at, v):
            act.wait_ge(done, at + 2)
            nc.scalar.activation(log_var[:, v:v + 1], moments[:, v, 1:2], ACT.Ln, bias=eps_col[:, 0:1]).then_inc(log_done, 1)
            act.wait_ge(log_done, log_at + 1)
            nc.scalar.activation(rstd[:, v:v + 1], log_var[:, v:v + 1], ACT.Exp, scale=-0.5).then_inc(inv_done, 1)

        def act_cut0(act, b, v):
            act.wait_ge(prod, b)
            for to, of, n in ((n_x, acc_x, D), (n_e, acc_e, D), (n_deg, acc_deg, 1)):
                last = nc.scalar.copy(to[0:n, v, :], of[0:n, bass.ds(BN * b, BN)])
            last.then_inc(cut, 1)

        def pe_products0(pe, b, v, turn):
            a, c = ps4[2 * v], ps4[2 * v + 1]
            pe.wait_ge(cut, b + 1)
            pe.wait_ge(x_in[v], DMA * (turn + 1))
            if there(b - 2):
                pe.wait_ge(q_steps, b - 1)
                pe.wait_ge(p_cp, b - 1)
            nc.tensor.matmul(a[:, 0:BN], waT, n_x[:, v, :], start=True, stop=False)
            nc.tensor.matmul(a[:, 0:BN], wbT, n_e[:, v, :], start=False, stop=False)
            nc.tensor.matmul(a[:, 0:BN], b_msg_row, n_deg[:, v, :], start=False, stop=True)
            nc.tensor.transpose(a[:, D:D + BN], x_blk[:, v, :], ident[0:BN, 0:BN])
            nc.tensor.matmul(c[0:BN, 3 * D:3 * D + 1], n_deg[:, v, :], ones[0:1, 0:1], start=True, stop=True).then_inc(prod, 1)

        def act_products0(act, b, v):
            act.wait_ge(prod, b + 1)
            if there(b - 2):
                act.wait_ge(mix, b - 1)
            nc.scalar.copy(hsT[:, v, :], ps4[2 * v][:, 0:BN])
            nc.scalar.copy(xT[:, v, :], ps4[2 * v][:, D:D + BN]).then_inc(prod_cp, 1)

        def pe_mix0(pe, b, v):
            c = ps4[2 * v + 1]
            pe.wait_ge(prod_cp, b + 1)
            nc.tensor.matmul(c[0:BN, 0:D], hsT[:, v, :], wdT, start=True, stop=True)
            nc.tensor.matmul(c[0:BN, D:2 * D], xT[:, v, :], wcT, start=True, stop=False)
            nc.tensor.matmul(c[0:BN, D:2 * D], ones[0:1, 0:BN], b_app_row, start=False, stop=True).then_inc(mix, 1)

        def dve_norm0(dve, b, v):
            c = ps4[2 * v + 1]
            dve.wait_ge(mix, b + 1)
            nc.vector.tensor_scalar(deg_max[:, v:v + 1], c[0:BN, 3 * D:3 * D + 1], 1.0, None, ALU.max).then_inc(deg_steps, 1)
            dve.wait_ge(deg_steps, 2 * b + 1)
            nc.vector.reciprocal(deg_inv[:, v:v + 1], deg_max[:, v:v + 1]).then_inc(deg_steps, 1)
            dve.wait_ge(deg_steps, 2 * b + 2)
            nc.vector.tensor_scalar(z[:, v, :], c[0:BN, 0:D], deg_inv[:, v:v + 1], None, ALU.mult).then_inc(ln0, 1)
            dve.wait_ge(ln0, LN0_STEPS * b + 1)
            nc.vector.tensor_tensor(z[:, v, :], z[:, v, :], c[0:BN, D:2 * D], ALU.add).then_inc(ln0, 1)
            dve.wait_ge(ln0, LN0_STEPS * b + 2)
            nc.vector.scalar_tensor_tensor(y[:, v, :], z[:, v, :], 0.0, x_blk[:, v, :], ALU.max, ALU.add).then_inc(ln0, 1)
            dve.wait_ge(ln0, LN0_STEPS * b + 3)
            if there(b - 2):
                dve.wait_ge(tab_out[v], DMA * (b - v))
            norm_steps(dve, ln0, LN0_STEPS * b + 3, rstd0, b, v, y[:, v, :], tab_blk[:, v, 0:D])

        def pe_turn0(pe, b, v):
            pe.wait_ge(ln0, LN0_STEPS * (b + 1))
            nc.tensor.transpose(ps4[2 * v + 1][:, 2 * D:2 * D + BN], tab_blk[:, v, 0:D], ident[0:BN, 0:BN]).then_inc(x1_tr, 1)

        def act_turn0(act, b, v):
            act.wait_ge(x1_tr, b + 1)
            if there(b - 2):
                act.wait_ge(pq, b - 1)
            nc.scalar.copy(x1T[:, v, :], ps4[2 * v + 1][:, 2 * D:2 * D + BN]).then_inc(x1_cp, 1)

        def pe_pq0(pe, b, v):
            a, c = ps4[2 * v], ps4[2 * v + 1]
            pe.wait_ge(x1_cp, b + 1)
            nc.tensor.matmul(c[0:BN, 0:D], x1T[:, v, :], w1_sb[:, 0:D], start=True, stop=False)
            nc.tensor.matmul(c[0:BN, 0:D], ones[0:1, 0:BN], b1_row, start=False, stop=True)
            nc.tensor.matmul(a[0:BN, 3 * D:4 * D], x1T[:, v, :], w1_sb[:, D:2 * D], start=True, stop=True).then_inc(pq, 1)

        def dve_parts0(dve, b, v):
            q = ps4[2 * v][0:BN, 3 * D:4 * D]
            hi, mid, lo = (q_blk[:, v, k * D:(k + 1) * D] for k in range(3))
            dve.wait_ge(pq, b + 1)
            if there(b - 2):
                dve.wait_ge(tab_out[v], DMA * (b - v))
            nc.vector.tensor_copy(hi, q).then_inc(q_split, 1)
            dve.wait_ge(q_split, 3 * b + 1)
            nc.vector.tensor_tensor(q_rest[:, v, 0, :], q, hi, ALU.subtract).then_inc(q_split, 1)
            dve.wait_ge(q_split, 3 * b + 2)
            nc.vector.tensor_copy(mid, q_rest[:, v, 0, :]).then_inc(q_split, 1)
            dve.wait_ge(q_split, 3 * b + 3)
            nc.vector.tensor_tensor(lo, q_rest[:, v, 0, :], mid, ALU.subtract).then_inc(q_steps, 1)

        def act_rstd0(act, b, v):
            act_rstd(act, ln0, LN0_STEPS * b + 3, rstd0, b, v)

        def act_store0(act, b, v):
            act.wait_ge(pq, b + 1)
            if there(b - 2):
                act.wait_ge(tab_out[v], DMA * (b - v))
            nc.scalar.copy(tab_blk[:, v, D:2 * D], ps4[2 * v + 1][0:BN, 0:D]).then_inc(p_cp, 1)
            act.wait_ge(p_cp, b + 1)
            act.wait_ge(q_steps, b + 1)
            act.dma_start(table[bass.ds(BN * b, BN), :], tab_blk[:, v, :]).then_inc(tab_out[v], DMA)
            act.dma_start(q_parts[bass.ds(BN * b, BN), :], q_blk[:, v, :]).then_inc(tab_out[v], DMA)

        def sp_x_block(sp, b, v, size=BN):
            if there(b - 2):
                wait_apart(sp, ln0, LN0_STEPS * (b - 2) + 3)
                sp.wait_ge(prod, b - 1)
            sp.dma_start(x_blk[0:size, v, :], x[bass.ds(BN * b, size), :]).then_inc(x_in[v], DMA)

        def act_cut1(act, b, v):
            act.wait_ge(sum_tr, b)
            nc.scalar.copy(n_x[:, v, :], acc_x[:, bass.ds(BN * b, BN)]).then_inc(cut1, 1)

        def pe_turn1(pe, b, v):
            pe.wait_ge(cut1, b + 1)
            if there(b - 2):
                pe.wait_ge(ln1, LN1_STEPS * (b - 2) + 1)
            nc.tensor.transpose(ps_fin[v][0:BN, 0:D], n_x[:, v, :], ident[:, :]).then_inc(sum_tr, 1)

        def dve_norm1(dve, b, v, turn):
            at = LN1_STEPS * b
            dve.wait_ge(sum_tr, b + 1)
            dve.wait_ge(x1_in[v], DMA * (turn + 1))
            nc.vector.tensor_tensor(z[:, v, :], ps_fin[v][0:BN, 0:D], x_blk[:, v, :], ALU.add).then_inc(ln1, 1)
            dve.wait_ge(ln1, at + 1)
            norm_steps(dve, ln1, at + 1, rstd1, 2 * b, v, z[:, v, :], y[:, v, :])
            dve.wait_ge(ln1, at + 4)
            nc.vector.tensor_tensor(z[:, v, :], y[:, v, :], gamma_bc[0:BN, :], ALU.mult).then_inc(ln1, 1)
            dve.wait_ge(ln1, at + 5)
            nc.vector.tensor_tensor(y[:, v, :], z[:, v, :], beta_bc[0:BN, :], ALU.add).then_inc(ln1, 1)
            dve.wait_ge(ln1, at + 6)
            nc.vector.tensor_tensor(z[:, v, :], y[:, v, :], x_blk[:, v, :], ALU.add).then_inc(ln1, 1)
            dve.wait_ge(ln1, at + 7)
            if there(b - 2):
                dve.wait_ge(fin_out[v], DMA // 2 * (b - v))
            norm_steps(dve, ln1, at + 7, rstd1, 2 * b + 1, v, z[:, v, :], fin[:, v, :])

        def act_rstd1(act, b, v):
            for k, after in enumerate((1, 7)):
                act_rstd(act, ln1, LN1_STEPS * b + after, rstd1, NB + 2 * b + k, v)

        def act_store1(act, b, v, size=BN):
            act.wait_ge(ln1, LN1_STEPS * (b + 1))
            act.dma_start(out[bass.ds(BN * b, size), :], fin[0:size, v, :]).then_inc(fin_out[v], DMA)

        def sp_x1_block(sp, b, v):
            if there(b - 2):
                sp.wait_ge(ln1, LN1_STEPS * (b - 2) + 7)
            sp.dma_start(x_blk[:, v, :], table[bass.ds(BN * b, BN), 0:D]).then_inc(x1_in[v], DMA)

        def accumulate(dve, psum_cols, into, at):
            return nc.vector.tensor_tensor(into[:, bass.ds(at, W)], into[:, bass.ds(at, W)], psum_cols, ALU.add)

        def tables_stored(eng):
            for v in range(2):
                eng.wait_ge(tab_out[v], NB * DMA)

        def weights(dve, u, g, first_bank):
            dve.wait_ge(h_done, g + 1)
            for j in range(TILES):
                cols = ps4[first_bank + j // 4][:, (j % 4) * D:(j % 4 + 1) * D]
                last = nc.vector.scalar_tensor_tensor(act_out[:, j, :], cols, 0.0, w2_bc, ALU.max, ALU.mult,
                                                      accum_out=logit[:, u, j:j + 1])
            last.then_inc(dot_done, 1)
            dve.wait_ge(sig_done, g + 1)
            nc.vector.tensor_scalar(expm1[:, u, :], expm[:, u, :], 1.0, None, ALU.add).then_inc(w_steps, 1)
            dve.wait_ge(w_steps, 2 * g + 1)
            nc.vector.reciprocal(weight[:, u, :], expm1[:, u, :]).then_inc(w_steps, 1)
            dve.wait_ge(w_steps, 2 * g + 2)

        def exp_logit(act, u, g):
            act.wait_ge(dot_done, g + 1)
            nc.scalar.activation(expm[:, u, :], logit[:, u, :], ACT.Exp, bias=b2_neg[:, 0:1], scale=-1.0).then_inc(sig_done, 1)

        def windowed():
            with nc.Block() as block:
                @block.sync
                def _(sp):
                    def load(i, u, last=False):
                        g = SLOTS * i + u
                        if there(i - 1):
                            sp.wait_ge(gath0[u], TILES * DMA * i)
                        if last:
                            sp.dma_start(src_slot[0:REST_P, u, :], src_rest).then_inc(src_in0[u], DMA)
                            sp.dma_start(src_slot[REST_P:REST_P + 1, u, 0:REST_J], src_end).then_inc(src_in0[u], DMA)
                        else:
                            sp.dma_start(src_slot[:, u, :], src_g[g]).then_inc(src_in0[u], DMA)
                        if there(i - 1):
                            sp.wait_ge(rel_done, g - SLOTS + 1)
                        if last:
                            sp.dma_start(dst_slot[:, u, :], no_node[:, :]).then_inc(pad_in, DMA)
                            sp.wait_ge(pad_in, DMA)
                            sp.dma_start(dst_slot[0:REST_P, u, :], dst_rest).then_inc(dst_in[u], DMA)
                            sp.dma_start(dst_slot[REST_P:REST_P + 1, u, 0:REST_J], dst_end).then_inc(dst_in[u], DMA)
                        else:
                            sp.dma_start(dst_slot[:, u, :], dst_g[g]).then_inc(dst_in[u], DMA)
                        if there(i - 1):
                            sp.wait_ge(agg0, g - SLOTS + 1)
                        if last:
                            sp.dma_start(ring[0:REST_P, u, GE:2 * GE], edge_rest).then_inc(edge_in[u], DMA)
                            sp.dma_start(ring[REST_P:REST_P + 1, u, GE:GE + REST_J * D], edge_end).then_inc(edge_in[u], DMA)
                        else:
                            sp.dma_start(ring[:, u, GE:2 * GE], edge_g[g]).then_inc(edge_in[u], DMA)
                        b, v = 2 * i + u // 2 - 1, 1 - u // 2
                        if u % 2 == 1 and there(b):
                            sp_x_block(sp, b, v)

                    for n in range(2 * SLOTS):
                        load(*divmod(n, SLOTS))
                    with sp.Fori(2, TURNS - 1) as i:
                        for u in range(SLOTS):
                            load(i, u)
                    for u in range(SLOTS):
                        load(TURNS - 1, u, last=u == SLOTS - 1)
                    sp_x_block(sp, NB - 1, 1, LAST_BN)

                @block.gpsimd
                def _(pool):
                    def gather(i, u):
                        g = SLOTS * i + u
                        pool.wait_ge(src_in0[u], DMA * (i + 1 + is_last(i, u)))
                        if there(i - 1):
                            wait_apart(pool, agg0, g - SLOTS + 1)
                        for j in range(TILES):
                            nc.gpsimd.indirect_dma_start(
                                out=ring[:, u, j * D:(j + 1) * D], out_offset=None, in_=x,
                                in_offset=bass.IndirectOffsetOnAxis(ap=src_slot[:, u, j:j + 1], axis=0),
                            ).then_inc(gath0[u], DMA)

                    for n in range(2 * SLOTS):
                        gather(*divmod(n, SLOTS))
                    with pool.Fori(2, TURNS - 1) as i:
                        for u in range(SLOTS):
                            gather(i, u)
                    for u in range(SLOTS):
                        gather(TURNS - 1, u)

                @block.vector
                def _(dve):
                    def sums(i, u):
                        g = SLOTS * i + u
                        at = dve.value_load(base_i[0:1, bass.ds(g, 1)], min_val=0, max_val=BASE_MAX)
                        dve.wait_ge(agg0, g + 1)
                        if there(g - 1):
                            dve.wait_ge(acc0, g)
                        ps = ps_agg[u % 2]
                        accumulate(dve, ps[:, 0:W], acc_x, at)
                        accumulate(dve, ps[:, W:2 * W], acc_e, at)
                        accumulate(dve, ps[0:1, 2 * W:3 * W], acc_deg, at).then_inc(acc0, 1)

                    def one_hots(i, u):
                        g = SLOTS * i + u
                        dve.wait_ge(dst_in[u], DMA * (i + 1 + is_last(i, u)))
                        nc.vector.tensor_scalar(rel[:, bass.ds(TILES * g, TILES)], dst_slot[:, u, :],
                                                base_bc[:, bass.ds(g, 1)], None, ALU.subtract).then_inc(rel_done, 1)
                        dve.wait_ge(rel_done, g + 1)
                        if there(i - 1):
                            dve.wait_ge(agg0, g - SLOTS + 1)
                        for j in range(TILES):
                            last = nc.vector.tensor_scalar(S[:, u, j, :], iota_w[:, :],
                                                           rel[:, bass.ds(TILES * g + j, 1)], None, ALU.is_equal)
                        last.then_inc(s_ready, 1)
                        dve.wait_ge(s_ready, g + 1)
                        nc.vector.tensor_reduce(S_sum[:, u, :], S[:, u, :, :].rearrange("p j w -> p w j"), AX_X,
                                                ALU.add).then_inc(sum_ready, 1)

                    def step(i, u):
                        if not is_last(i, u):
                            one_hots(*ahead(i, u))
                        before = back(i, u, 1)
                        if there(before[0]):
                            sums(*before)
                        b, v = 2 * i + u // 2 - 2, u // 2
                        if u % 2 == 0 and there(b - 1):
                            dve_parts0(dve, b - 1, 1 - v)
                        if u % 2 == 1 and there(b):
                            dve_norm0(dve, b, v)

                    one_hots(0, 0)
                    for n in range(2 * SLOTS):
                        step(*divmod(n, SLOTS))
                    with dve.Fori(2, TURNS - 1) as i:
                        for u in range(SLOTS):
                            step(i, u)
                    for u in range(SLOTS):
                        step(TURNS - 1, u)
                    sums(TURNS - 1, SLOTS - 1)
                    dve_parts0(dve, NB - 3, 1)
                    dve_norm0(dve, NB - 2, 0)
                    dve_norm0(dve, NB - 1, 1)
                    dve_parts0(dve, NB - 2, 0)
                    dve_parts0(dve, NB - 1, 1)
                    dve.wait_ge(cut, NB)
                    nc.vector.memset(acc_x[:, :], 0.0).then_inc(cleared, 1)

                @block.tensor
                def _(pe):
                    def summed(u, at, lhs_at):
                        for j in range(TILES):
                            nc.tensor.matmul(ps_agg[u % 2][:, at:at + W],
                                             ring[:, u, lhs_at + j * D:lhs_at + (j + 1) * D], S[:, u, j, :],
                                             start=j == 0, stop=j == TILES - 1)

                    def step(i, u):
                        g = SLOTS * i + u
                        b, v = 2 * i + u // 2 - 2, u // 2
                        pe.wait_ge(gath0[u], TILES * DMA * (i + 1))
                        pe.wait_ge(s_ready, g + 1)
                        if there(g - 2):
                            pe.wait_ge(acc0, g - 1)
                        summed(u, 0, 0)
                        if u % 2 == 0 and there(b - 1):
                            pe_pq0(pe, b - 1, 1 - v)
                        if u % 2 == 0 and there(b):
                            pe_products0(pe, b, v, i - 1)
                        pe.wait_ge(edge_in[u], DMA * (i + 1 + is_last(i, u)))
                        summed(u, W, GE)
                        pe.wait_ge(sum_ready, g + 1)
                        nc.tensor.matmul(ps_agg[u % 2][0:1, 2 * W:3 * W], ones[:, 0:1], S_sum[:, u, :], start=True,
                                         stop=True).then_inc(agg0, 1)
                        if u % 2 == 0 and there(b):
                            pe_mix0(pe, b, v)
                        if u % 2 == 1 and there(b):
                            pe_turn0(pe, b, v)

                    for n in range(2 * SLOTS):
                        step(*divmod(n, SLOTS))
                    with pe.Fori(2, TURNS - 1) as i:
                        for u in range(SLOTS):
                            step(i, u)
                    for u in range(SLOTS):
                        step(TURNS - 1, u)
                    pe_pq0(pe, NB - 3, 1)
                    for phase in (lambda b, v: pe_products0(pe, b, v, TURNS - 1), lambda b, v: pe_mix0(pe, b, v),
                                  lambda b, v: pe_turn0(pe, b, v), lambda b, v: pe_pq0(pe, b, v)):
                        phase(NB - 2, 0)
                        phase(NB - 1, 1)

                @block.scalar
                def _(act):
                    def step(i, u):
                        b, v = 2 * i + u // 2 - 2, u // 2
                        if u % 2 == 0 and there(b):
                            act.wait_ge(acc0, 2 * b + LAG0)
                            act_cut0(act, b, v)
                            act_products0(act, b, v)
                        if u % 2 == 0 and there(b - 1):
                            act_store0(act, b - 1, 1 - v)
                        if u % 2 == 1 and there(b):
                            act_rstd0(act, b, v)
                            act_turn0(act, b, v)

                    for n in range(2 * SLOTS):
                        step(*divmod(n, SLOTS))
                    with act.Fori(2, TURNS) as i:
                        for u in range(SLOTS):
                            step(i, u)
                    act_store0(act, NB - 3, 1)
                    act.wait_ge(acc0, G)
                    for phase in (act_cut0, act_products0, act_rstd0, act_turn0, act_store0):
                        phase(act, NB - 2, 0)
                        phase(act, NB - 1, 1)
                    tables_stored(act)

            with nc.Block() as block:
                @block.sync
                def _(sp):
                    def load(i, u, last=False):
                        g = SLOTS * i + u
                        if there(i - 1):
                            sp.wait_ge(gath1[u], TILES * DMA * i)
                        if last:
                            sp.dma_start(src_slot[0:REST_P, u, :], src_rest).then_inc(src_in1[u], DMA)
                            sp.dma_start(src_slot[REST_P:REST_P + 1, u, 0:REST_J], src_end).then_inc(src_in1[u], DMA)
                        else:
                            sp.dma_start(src_slot[:, u, :], src_g[g]).then_inc(src_in1[u], DMA)
                        if there(i - 1):
                            wait_apart(sp, st_ready, g - SLOTS + 1)
                        sp.dma_start(rel_bc[:, u, :], rel_rows[bass.ds(g, 1), :].to_broadcast([P, GE])).then_inc(row_in[u], DMA)
                        at = sp.value_load(base_i[0:1, bass.ds(g, 1)], min_val=0, max_val=BASE_MAX)
                        if there(i - 1):
                            sp.wait_ge(h_done, g - SLOTS + 1)
                        sp.dma_start(q_win[:, u, :], q_parts[bass.ds(at, W), :]).then_inc(q_in[u], DMA)
                        b, v = 2 * i + u // 2 - 1, 1 - u // 2
                        if u % 2 == 1 and there(b):
                            sp_x1_block(sp, b, v)

                    for n in range(2 * SLOTS):
                        load(*divmod(n, SLOTS))
                    with sp.Fori(2, TURNS - 1) as i:
                        for u in range(SLOTS):
                            load(i, u)
                    for u in range(SLOTS):
                        load(TURNS - 1, u, last=u == SLOTS - 1)
                    sp_x1_block(sp, NB - 1, 1)

                @block.gpsimd
                def _(pool):
                    def gather(i, u):
                        g = SLOTS * i + u
                        pool.wait_ge(src_in1[u], DMA * (i + 1 + is_last(i, u)))
                        if there(i - 1):
                            wait_apart(pool, agg1, g - SLOTS + 1)
                        for j in range(TILES):
                            nc.gpsimd.indirect_dma_start(
                                out=ring[:, u, 2 * j * D:2 * (j + 1) * D], out_offset=None, in_=table,
                                in_offset=bass.IndirectOffsetOnAxis(ap=src_slot[:, u, j:j + 1], axis=0),
                            ).then_inc(gath1[u], DMA)

                    for n in range(2 * SLOTS):
                        gather(*divmod(n, SLOTS))
                    with pool.Fori(2, TURNS - 1) as i:
                        for u in range(SLOTS):
                            gather(i, u)
                    for u in range(SLOTS):
                        gather(TURNS - 1, u)

                @block.vector
                def _(dve):
                    def sums(i, u):
                        g = SLOTS * i + u
                        at = dve.value_load(base_i[0:1, bass.ds(g, 1)], min_val=0, max_val=BASE_MAX)
                        dve.wait_ge(agg1, g + 1)
                        if there(g - 1):
                            dve.wait_ge(acc1, g)
                        accumulate(dve, ps_agg[u % 2][:, 0:W], acc_x, at).then_inc(acc1, 1)

                    def one_hots(i, u):
                        g = SLOTS * i + u
                        dve.wait_ge(row_in[u], DMA * (i + 1))
                        if there(i - 1):
                            dve.wait_ge(h_done, g - SLOTS + 1)
                        nc.vector.tensor_scalar(ST[:, u, :, :].rearrange("w j p -> w p j"),
                                                rel_bc[:, u, :].rearrange("w (p j) -> w p j", j=TILES),
                                                iota_p[:, 0:1], None, ALU.is_equal).then_inc(st_ready, 1)

                    def step(i, u):
                        if not is_last(i, u):
                            one_hots(*ahead(i, u))
                        two_before, before = back(i, u, 2), back(i, u, 1)
                        if there(two_before[0]):
                            sums(*two_before)
                        if there(before[0]):
                            weigh(*before)
                        b, v = 2 * i + u // 2 - 2, u // 2
                        if u % 2 == 1 and there(b):
                            dve_norm1(dve, b, v, i - 1)

                    def weigh(i, u):
                        g = SLOTS * i + u
                        weights(dve, u, g, 2 * (u % 2))
                        if there(i - 1):
                            dve.wait_ge(agg1, g - SLOTS + 1)
                        for j in range(TILES):
                            last = nc.vector.tensor_scalar(S[:, u, j, :], iota_w[:, :], rel[:, bass.ds(TILES * g + j, 1)],
                                                           weight[:, u, j:j + 1], ALU.is_equal, ALU.mult)
                        last.then_inc(sw_ready, 1)

                    one_hots(0, 0)
                    for n in range(2 * SLOTS):
                        step(*divmod(n, SLOTS))
                    with dve.Fori(2, TURNS - 1) as i:
                        for u in range(SLOTS):
                            step(i, u)
                    for u in range(SLOTS):
                        step(TURNS - 1, u)
                    sums(TURNS - 1, SLOTS - 2)
                    weigh(TURNS - 1, SLOTS - 1)
                    sums(TURNS - 1, SLOTS - 1)
                    dve_norm1(dve, NB - 2, 0, TURNS - 1)
                    dve_norm1(dve, NB - 1, 1, TURNS - 1)

                @block.tensor
                def _(pe):
                    def pre_activation(i, u):
                        g = SLOTS * i + u
                        pe.wait_ge(gath1[u], TILES * DMA * (i + 1))
                        pe.wait_ge(q_in[u], DMA * (i + 1))
                        pe.wait_ge(st_ready, g + 1)
                        if there(g - 2):
                            pe.wait_ge(dot_done, g - 1)
                        for j in range(TILES):
                            cols = ps4[2 * (u % 2) + j // 4][:, (j % 4) * D:(j % 4 + 1) * D]
                            nc.tensor.matmul(cols, ident[:, :], ring[:, u, (2 * j + 1) * D:(2 * j + 2) * D], start=True, stop=False)
                            for k in range(3):
                                last = nc.tensor.matmul(cols, ST[:, u, j, :], q_win[:, u, k * D:(k + 1) * D],
                                                        start=False, stop=k == 2)
                        last.then_inc(h_done, 1)

                    def summed(i, u):
                        g = SLOTS * i + u
                        pe.wait_ge(sw_ready, g + 1)
                        if there(g - 2):
                            pe.wait_ge(acc1, g - 1)
                        for j in range(TILES):
                            last = nc.tensor.matmul(ps_agg[u % 2][:, 0:W], ring[:, u, 2 * j * D:(2 * j + 1) * D],
                                                    S[:, u, j, :], start=j == 0, stop=j == TILES - 1)
                        last.then_inc(agg1, 1)

                    def step(i, u):
                        b, v = 2 * i + u // 2 - 2, u // 2
                        pre_activation(i, u)
                        if u % 2 == 1 and there(b):
                            pe_turn1(pe, b, v)
                        before = back(i, u, 1)
                        if there(before[0]):
                            summed(*before)

                    for n in range(2 * SLOTS):
                        step(*divmod(n, SLOTS))
                    with pe.Fori(2, TURNS) as i:
                        for u in range(SLOTS):
                            step(i, u)
                    summed(TURNS - 1, SLOTS - 1)
                    pe_turn1(pe, NB - 2, 0)
                    pe_turn1(pe, NB - 1, 1)

                @block.scalar
                def _(act):
                    def step(i, u):
                        b, v = 2 * i + u // 2 - 2, u // 2
                        if u % 2 == 1 and there(b):
                            act.wait_ge(acc1, 2 * b + LAG0)
                            act_cut1(act, b, v)
                        before = back(i, u, 1)
                        if there(before[0]):
                            exp_logit(act, before[1], SLOTS * before[0] + before[1])
                        if u % 2 == 1 and there(b):
                            act_rstd1(act, b, v)
                            act_store1(act, b, v)

                    for n in range(2 * SLOTS):
                        step(*divmod(n, SLOTS))
                    with act.Fori(2, TURNS) as i:
                        for u in range(SLOTS):
                            step(i, u)
                    exp_logit(act, SLOTS - 1, G - 1)
                    act.wait_ge(acc1, G)
                    act_cut1(act, NB - 2, 0)
                    act_cut1(act, NB - 1, 1)
                    act_rstd1(act, NB - 2, 0)
                    act_rstd1(act, NB - 1, 1)
                    act_store1(act, NB - 2, 0)
                    act_store1(act, NB - 1, 1, LAST_BN)
                    for v in range(2):
                        act.wait_ge(fin_out[v], DMA * NB // 2)

        def general():
            def groups(eng, step):
                with eng.Fori(0, G - 1) as g:
                    step(g, False)
                step(G - 1, True)

            def blocks(eng, step):
                for v in range(2):
                    step(v, v, 0)
                with eng.Fori(1, NB // 2 - 1) as t:
                    for v in range(2):
                        step(2 * t + v, v, t)
                for v in range(2):
                    step(NB - 2 + v, v, NB // 2 - 1)

            def load_indices(sp, g, last, acc, src_in):
                sp.wait_ge(acc, WINDOWS * g + 1)
                if last:
                    sp.dma_start(src_slot[0:REST_P, 0, :], src_rest).then_inc(src_in, DMA)
                    sp.dma_start(src_slot[REST_P:REST_P + 1, 0, 0:REST_J], src_end).then_inc(src_in, DMA)
                    sp.dma_start(dst_slot[:, 0, :], no_node[:, :]).then_inc(pad_in, DMA)
                    sp.wait_ge(pad_in, DMA if acc is acc0 else 2 * DMA)
                    sp.dma_start(dst_slot[0:REST_P, 0, :], dst_rest).then_inc(dst_in[0], DMA)
                    sp.dma_start(dst_slot[REST_P:REST_P + 1, 0, 0:REST_J], dst_end).then_inc(dst_in[0], DMA)
                else:
                    sp.dma_start(src_slot[:, 0, :], src_g[g]).then_inc(src_in, DMA)
                    sp.dma_start(dst_slot[:, 0, :], dst_g[g]).then_inc(dst_in[0], DMA)

            def start_windows(dve, g, last, groups_before):
                dve.wait_ge(dst_in[0], DMA * (groups_before + g + 1 + last))
                nc.vector.tensor_scalar(rel[:, 0:TILES], dst_slot[:, 0, :], float(W), None, ALU.add).then_inc(rel_done, 1)

            def next_window(dve, n):
                dve.wait_ge(rel_done, n)
                nc.vector.tensor_scalar(rel[:, 0:TILES], rel[:, 0:TILES], float(-W), None, ALU.add).then_inc(rel_done, 1)
                dve.wait_ge(rel_done, n + 1)

            REL_STEPS = WINDOWS + 1
            L1_REL = G * REL_STEPS

            with nc.Block() as block:
                @block.sync
                def _(sp):
                    def step(g, last):
                        load_indices(sp, g, last, acc0, src_in0[0])
                        if last:
                            sp.dma_start(ring[0:REST_P, 0, GE:2 * GE], edge_rest).then_inc(edge_in[0], DMA)
                            sp.dma_start(ring[REST_P:REST_P + 1, 0, GE:GE + REST_J * D], edge_end).then_inc(edge_in[0], DMA)
                        else:
                            sp.dma_start(ring[:, 0, GE:2 * GE], edge_g[g]).then_inc(edge_in[0], DMA)

                    groups(sp, step)

                @block.gpsimd
                def _(pool):
                    def step(g, last):
                        wait_apart(pool, src_in0[0], DMA * (g + 1 + last))
                        wait_apart(pool, acc0, WINDOWS * g + 1)
                        for j in range(TILES):
                            nc.gpsimd.indirect_dma_start(
                                out=ring[:, 0, j * D:(j + 1) * D], out_offset=None, in_=x,
                                in_offset=bass.IndirectOffsetOnAxis(ap=src_slot[:, 0, j:j + 1], axis=0),
                            ).then_inc(gath0[0], DMA)

                    groups(pool, step)

                @block.vector
                def _(dve):
                    def step(g, last):
                        start_windows(dve, g, last, 0)
                        with dve.Fori(0, WINDOWS) as k:
                            n = WINDOWS * g + k
                            next_window(dve, REL_STEPS * g + k + 1)
                            for j in range(TILES):
                                done = nc.vector.tensor_scalar(S[:, 0, j, :], iota_w[:, :], rel[:, j:j + 1], None, ALU.is_equal)
                            done.then_inc(s_ready, 1)
                            dve.wait_ge(s_ready, n + 1)
                            nc.vector.tensor_reduce(S_sum[:, 0, :], S[:, 0, :, :].rearrange("p j w -> p w j"), AX_X,
                                                    ALU.add).then_inc(sum_ready, 1)
                            dve.wait_ge(agg0, n + 1)
                            dve.wait_ge(acc0, n + 1)
                            accumulate(dve, ps_agg[0][:, 0:W], acc_x, W * k)
                            accumulate(dve, ps_agg[0][:, W:2 * W], acc_e, W * k)
                            accumulate(dve, ps_agg[0][0:1, 2 * W:3 * W], acc_deg, W * k).then_inc(acc0, 1)

                    nc.vector.memset(acc_x[:, :], 0.0).then_inc(acc0, 1)
                    groups(dve, step)

                @block.tensor
                def _(pe):
                    def step(g, last):
                        pe.wait_ge(gath0[0], TILES * DMA * (g + 1))
                        wait_apart(pe, edge_in[0], DMA * (g + 1 + last))
                        with pe.Fori(0, WINDOWS) as k:
                            n = WINDOWS * g + k
                            pe.wait_ge(s_ready, n + 1)
                            pe.wait_ge(acc0, n + 1)
                            for at, lhs_at in ((0, 0), (W, GE)):
                                for j in range(TILES):
                                    nc.tensor.matmul(ps_agg[0][:, at:at + W], ring[:, 0, lhs_at + j * D:lhs_at + (j + 1) * D],
                                                     S[:, 0, j, :], start=j == 0, stop=j == TILES - 1)
                            pe.wait_ge(sum_ready, n + 1)
                            nc.tensor.matmul(ps_agg[0][0:1, 2 * W:3 * W], ones[:, 0:1], S_sum[:, 0, :], start=True,
                                             stop=True).then_inc(agg0, 1)

                    groups(pe, step)

            with nc.Block() as block:
                @block.sync
                def _(sp):
                    blocks(sp, lambda b, v, t: sp_x_block(sp, b, v, LAST_BN if isinstance(b, int) and b == NB - 1 else BN))

                @block.vector
                def _(dve):
                    def step(b, v, t):
                        dve_norm0(dve, b, v)
                        dve_parts0(dve, b, v)

                    blocks(dve, step)

                @block.tensor
                def _(pe):
                    def step(b, v, t):
                        pe_products0(pe, b, v, t)
                        pe_mix0(pe, b, v)
                        pe_turn0(pe, b, v)
                        pe_pq0(pe, b, v)

                    blocks(pe, step)

                @block.scalar
                def _(act):
                    def step(b, v, t):
                        act_cut0(act, b, v)
                        act_products0(act, b, v)
                        act_rstd0(act, b, v)
                        act_turn0(act, b, v)
                        act_store0(act, b, v)

                    act.wait_ge(acc0, WINDOWS * G + 1)
                    blocks(act, step)
                    tables_stored(act)

            with nc.Block() as block:
                @block.sync
                def _(sp):
                    def step(g, last):
                        load_indices(sp, g, last, acc1, src_in1[0])
                        if last:
                            sp.dma_start(dst_slot[0:REST_P, 1, :], dst_rest).then_inc(row_in[0], DMA)
                            sp.dma_start(dst_slot[REST_P:REST_P + 1, 1, 0:REST_J], dst_end).then_inc(row_in[0], DMA)
                        else:
                            sp.dma_start(dst_slot[:, 1, :], dst_g[g]).then_inc(row_in[0], DMA)

                    groups(sp, step)

                @block.gpsimd
                def _(pool):
                    def step(g, last):
                        wait_apart(pool, src_in1[0], DMA * (g + 1 + last))
                        wait_apart(pool, row_in[0], DMA * (g + 1 + last))
                        wait_apart(pool, acc1, WINDOWS * g + 1)
                        for j in range(TILES):
                            nc.gpsimd.indirect_dma_start(
                                out=ring[:, 0, 2 * j * D:2 * (j + 1) * D], out_offset=None, in_=table,
                                in_offset=bass.IndirectOffsetOnAxis(ap=src_slot[:, 0, j:j + 1], axis=0),
                            ).then_inc(gath1[0], DMA)
                            nc.gpsimd.indirect_dma_start(
                                out=q_rows[:, 3 * j * D:3 * (j + 1) * D], out_offset=None, in_=q_parts,
                                in_offset=bass.IndirectOffsetOnAxis(ap=dst_slot[:, 1, j:j + 1], axis=0),
                            ).then_inc(gath1[1], DMA)

                    groups(pool, step)

                @block.vector
                def _(dve):
                    def step(g, last):
                        start_windows(dve, g, last, G + 1)
                        weights(dve, 0, g, 0)
                        dve.sem_inc(passed, 1)
                        with dve.Fori(0, WINDOWS) as k:
                            n = WINDOWS * g + k
                            next_window(dve, REL_STEPS * g + k + L1_REL + 1)
                            for j in range(TILES):
                                done = nc.vector.tensor_scalar(S[:, 0, j, :], iota_w[:, :], rel[:, j:j + 1],
                                                               weight[:, 0, j:j + 1], ALU.is_equal, ALU.mult)
                            done.then_inc(sw_ready, 1)
                            dve.wait_ge(agg1, n + 1)
                            dve.wait_ge(acc1, n + 1)
                            accumulate(dve, ps_agg[0][:, 0:W], acc_x, W * k).then_inc(acc1, 1)

                    nc.vector.memset(acc_x[:, :], 0.0).then_inc(acc1, 1)
                    groups(dve, step)

                @block.tensor
                def _(pe):
                    def step(g, last):
                        pe.wait_ge(gath1[0], TILES * DMA * (g + 1))
                        pe.wait_ge(gath1[1], TILES * DMA * (g + 1))
                        pe.wait_ge(acc1, WINDOWS * g + 1)
                        for j in range(TILES):
                            cols = ps4[j // 4][:, (j % 4) * D:(j % 4 + 1) * D]
                            nc.tensor.matmul(cols, ident[:, :], ring[:, 0, (2 * j + 1) * D:(2 * j + 2) * D], start=True, stop=False)
                            for k in range(3):
                                done = nc.tensor.matmul(cols, identb[:, :], q_rows[:, (3 * j + k) * D:(3 * j + k + 1) * D],
                                                        start=False, stop=k == 2)
                        done.then_inc(h_done, 1)
                        with pe.Fori(0, WINDOWS) as k:
                            n = WINDOWS * g + k
                            pe.wait_ge(sw_ready, n + 1)
                            pe.wait_ge(acc1, n + 1)
                            for j in range(TILES):
                                done = nc.tensor.matmul(ps_agg[0][:, 0:W], ring[:, 0, 2 * j * D:(2 * j + 1) * D], S[:, 0, j, :],
                                                        start=j == 0, stop=j == TILES - 1)
                            done.then_inc(agg1, 1)

                    groups(pe, step)

                @block.scalar
                def _(act):
                    groups(act, lambda g, last: exp_logit(act, 0, g))

            with nc.Block() as block:
                @block.sync
                def _(sp):
                    blocks(sp, lambda b, v, t: sp_x1_block(sp, b, v))

                @block.vector
                def _(dve):
                    blocks(dve, lambda b, v, t: dve_norm1(dve, b, v, t))

                @block.tensor
                def _(pe):
                    blocks(pe, lambda b, v, t: pe_turn1(pe, b, v))

                @block.scalar
                def _(act):
                    def step(b, v, t):
                        act_cut1(act, b, v)
                        act_rstd1(act, b, v)
                        act_store1(act, b, v, LAST_BN if isinstance(b, int) and b == NB - 1 else BN)

                    act.wait_ge(acc1, WINDOWS * G + 1)
                    blocks(act, step)
                    for v in range(2):
                        act.wait_ge(fin_out[v], DMA * NB // 2)

        with nc.If(fitting == G):
            windowed()
        with nc.Else():
            general()


_INS = ['x', 'src', 'dst', 'edge_attr_128', 'L0_gnn_W_msg_w', 'L0_gnn_W_msg_b', 'L0_gnn_W_app_w', 'L0_gnn_W_app_b',
        'L1_gnn_W1', 'L1_gnn_b1', 'L1_gnn_W2', 'L1_gnn_b2', 'L1_gnn_gamma', 'L1_gnn_beta']


def kernel(**inputs):
    import numpy as _np
    import concourse.bacc as _bacc
    from concourse import mybir as _mybir
    from concourse.bass_utils import run_bass_kernel_spmd as _run

    nc = _bacc.Bacc("TRN2", target_bir_lowering=False, num_devices=1)
    arrays, args = {}, []
    for name in _INS:
        a = _np.ascontiguousarray(inputs[name])
        arrays[f"in_{name}_dram"] = a
        args.append(nc.dram_tensor(f"in_{name}_dram", a.shape, _mybir.dt.from_np(a.dtype), kind="ExternalInput").ap())
    args.append(nc.dram_tensor("out_0_dram", (N, D), F32, kind="ExternalOutput").ap())
    build(nc, *args)
    r = _run(nc, [arrays], core_ids=[0])
    return r.results[0]["out_0_dram"]
```

```python
import concourse.bass as bass
from concourse import mybir
from contextlib import ExitStack

F32 = mybir.dt.float32
BF16 = mybir.dt.bfloat16
I32 = mybir.dt.int32
ALU = mybir.AluOpType
ACT = mybir.ActivationFunctionType
AX_X = mybir.AxisListType.X

E, N, D = 106250, 6250, 128
P = 128
TILES = 8
GE = P * TILES
G = -(-E // GE)
FULL = E // GE
REST = E - FULL * GE
REST_P, REST_J = REST // TILES, REST % TILES
SLOTS = 4
TURNS = G // SLOTS
PEELED = 3
W = 128
NB = G // 2
BN = -(-N // NB)
NPAD = NB * BN
LAST_BN = N - (NB - 1) * BN
BASE_MAX = NPAD - W
EPS = 1e-5
NO_NODE = 30000
DMA = 16
LN0_STEPS, LN1_STEPS = 7, 12
WINDOWS = -(-NPAD // W)


def back(i, u, d):
    return i + (u - d) // SLOTS, (u - d) % SLOTS


def ahead(i, u):
    return i + (u + 1) // SLOTS, (u + 1) % SLOTS


def there(i):
    return not isinstance(i, int) or i >= 0


def block_back(i, u, d):
    half = u // 2 - d
    return i + half // 2, half % 2


def is_last(i, u):
    return isinstance(i, int) and SLOTS * i + u == G - 1


def build(nc, x, src, dst, edge, w_msg, b_msg, w_app, b_app, w1, b1, w2, b2, gamma, beta, out):
    ctx = ExitStack()

    def sb(name, shape, dt=F32):
        return ctx.enter_context(nc.sbuf_tensor(name, shape, dt))

    def sem(name):
        return ctx.enter_context(nc.semaphore(name))

    def sems(name, n):
        return [sem(f"{name}{k}") for k in range(n)]

    with ctx:
        table = nc.dram_tensor("table", (NPAD, 2 * D), F32, kind="Internal").ap()
        q_parts = nc.dram_tensor("q_parts", (NPAD, 3 * D), BF16, kind="Internal").ap()
        rel_rows = nc.dram_tensor("rel_rows", (G, GE), BF16, kind="Internal").ap()

        src_g = src[0:FULL * GE].rearrange("(g p j) -> g p j", p=P, j=TILES)
        dst_g = dst[0:FULL * GE].rearrange("(g p j) -> g p j", p=P, j=TILES)
        edge_g = edge[0:FULL * GE, :].rearrange("(g p j) d -> g p (j d)", p=P, j=TILES)
        src_rest, dst_rest = (a[FULL * GE:FULL * GE + REST_P * TILES].rearrange("(p j) -> p j", j=TILES)
                              for a in (src, dst))
        edge_rest = edge[FULL * GE:FULL * GE + REST_P * TILES, :].rearrange("(p j) d -> p (j d)", j=TILES)
        src_end, dst_end = (a[E - REST_J:E].rearrange("(p j) -> p j", p=1) for a in (src, dst))
        edge_end = edge[E - REST_J:E, :].rearrange("(p j) d -> p (j d)", p=1)

        ident = sb("ident", [P, P])
        identb = sb("identb", [P, P], BF16)
        ones = sb("ones", [P, P])
        iota_w = sb("iota_w", [P, W])
        iota_i = sb("iota_i", [P, W], I32)
        iota_pi = sb("iota_pi", [P, 1], I32)
        iota_p = sb("iota_p", [P, 1])
        wmsg_sb = sb("wmsg_sb", [D, 2 * D])
        wapp_sb = sb("wapp_sb", [D, 2 * D])
        wT = sb("wT", [D, 4, D])
        w1_sb = sb("w1_sb", [D, 2 * D])
        rows = sb("rows", [1, 6 * D])
        b2_row = sb("b2_row", [1, 1])
        bcast = sb("bcast", [P, 3, D])
        b2_col = sb("b2_col", [P, 1])
        dst_nat = sb("dst_nat", [G, GE], I32)
        dst_f = sb("dst_f", [G, GE])
        rel_nat = sb("rel_nat", [G, GE], BF16)
        low = sb("low", [G, 1])
        high = sb("high", [G, 1])
        base = sb("base", [G, 1])
        floor_i = sb("floor_i", [G, 1], I32)
        floor = sb("floor", [G, 1])
        spread = sb("spread", [G, 1])
        fits = sb("fits", [G, 2])
        ok = sb("ok", [G, 1])
        base_l = sb("base_l", [G, P])
        base_bc = sb("base_bc", [P, G])
        base_i = sb("base_i", [1, G], I32)
        ok_i = sb("ok_i", [1, 1], I32)
        no_node = sb("no_node", [P, TILES], I32)

        src_slot = sb("src_slot", [P, SLOTS, TILES], I32)
        dst_slot = sb("dst_slot", [P, SLOTS, TILES], I32)
        rel = sb("rel", [P, G * TILES])
        ring = sb("ring", [P, SLOTS, 2 * GE])
        S = sb("S", [P, SLOTS, TILES, W])
        S_sum = sb("S_sum", [P, SLOTS, W])
        acc_x = sb("acc_x", [D, WINDOWS * W])
        acc_e = sb("acc_e", [D, WINDOWS * W])
        acc_deg = sb("acc_deg", [1, WINDOWS * W])
        x_blk = sb("x_blk", [BN, 2, D])
        n_x = sb("n_x", [D, 2, BN])
        n_e = sb("n_e", [D, 2, BN])
        n_deg = sb("n_deg", [1, 2, BN])
        hsT = sb("hsT", [D, 2, BN])
        xT = sb("xT", [D, 2, BN])
        x1T = sb("x1T", [D, 2, BN])
        deg_max = sb("deg_max", [BN, 2])
        deg_inv = sb("deg_inv", [BN, 2])
        z = sb("z", [BN, 2, D])
        y = sb("y", [BN, 2, D])
        stats = sb("stats", [BN, 2, 6])
        moments = sb("moments", [BN, 2, 2])
        std = sb("std", [BN, 2])
        rstd = sb("rstd", [BN, 2])
        eps_col = sb("eps_col", [BN, 1])
        tab_blk = sb("tab_blk", [BN, 2, 2 * D])
        q_blk = sb("q_blk", [BN, 2, 3 * D], BF16)
        q_rest = sb("q_rest", [BN, 2, 2, D])
        rel_bc = sb("rel_bc", [P, SLOTS, GE], BF16)
        ST = sb("ST", [P, SLOTS, TILES, P], BF16)
        q_win = sb("q_win", [P, SLOTS, 3 * D], BF16)
        act_out = sb("act_out", [P, TILES, D])
        logit = sb("logit", [P, SLOTS, TILES])
        weight = sb("weight", [P, SLOTS, TILES])
        fin = sb("fin", [BN, 2, D])
        q_rows = ST[:, :, :, :].rearrange("p s t c -> p (s t c)")[:, 0:3 * GE]

        def bank(name):
            return ctx.enter_context(nc.psum_tensor(name, [P, 512], F32))

        ps_agg = [bank("ps_agg0"), bank("ps_agg1")]
        ps4 = [bank(f"ps4_{k}") for k in range(4)]
        ps_fin = [bank("ps_fin0"), bank("ps_fin1")]

        ld_dst, ld_par, memset_ok, iota_ok = sem("ld_dst"), sem("ld_par"), sem("memset_ok"), sem("iota_ok")
        ident_ok, dve_pro, pe_pro, act_pro = sem("ident_ok"), sem("dve_pro"), sem("pe_pro"), sem("act_pro")
        rel_out = sem("rel_out")
        src_in0, dst_in, edge_in, gath0 = sems("src_in0_", 4), sems("dst_in", 4), sems("edge_in", 4), sems("gath0_", 4)
        pad_in = sem("pad_in")
        rel_done, s_ready, sum_ready, agg0, acc0 = (sem(n) for n in ("rel_done", "s_ready", "sum_ready", "agg0", "acc0"))
        x_in = sems("x_in", 2)
        cut, prod, prod_cp, deg_steps, mix = (sem(n) for n in ("cut", "prod", "prod_cp", "deg_steps", "mix"))
        x1_tr, x1_cp, pq, p_cp, parts = (sem(n) for n in ("x1_tr", "x1_cp", "pq", "p_cp", "parts"))
        q_split, ln0, root0, ln1, root1 = sem("q_split"), *(sems(n, 2) for n in ("ln0_", "root0_", "ln1_", "root1_"))
        tab_out = sems("tab_out", 2)
        cleared = sem("cleared")
        src_in1, gath1, row_in, q_in = sems("src_in1_", 4), sems("gath1_", 4), sems("row_in", 4), sems("q_in", 4)
        st_ready, h_done, dot_done, sig_done, sw_ready, agg1, acc1 = (
            sem(n) for n in ("st_ready", "h_done", "dot_done", "sig_done", "sw_ready", "agg1", "acc1"))
        x1_in, cut1, sum_tr = sems("x1_in", 2), sem("cut1"), sem("sum_tr")
        fin_out, passed = sems("fin_out", 2), sem("passed")

        pro = nc.Block()
        with pro as block:
            @block.sync
            def _(sp):
                sp.wait_ge(memset_ok, 1)
                sp.dma_start(dst_nat[0:FULL, :], dst[0:FULL * GE].rearrange("(g e) -> g e", e=GE)).then_inc(ld_dst, DMA)
                sp.dma_start(dst_nat[FULL:G, 0:REST], dst[FULL * GE:E].rearrange("(g e) -> g e", g=1)).then_inc(ld_dst, DMA)
                sp.dma_start(wmsg_sb[:, :], w_msg).then_inc(ld_par, DMA)
                sp.dma_start(wapp_sb[:, :], w_app).then_inc(ld_par, DMA)
                for k in range(2):
                    sp.dma_start(w1_sb[:, k * D:(k + 1) * D], w1[k * D:(k + 1) * D, :]).then_inc(ld_par, DMA)
                for k, v in enumerate((b_msg, b_app, b1, w2.rearrange("f o -> (f o)"), gamma, beta)):
                    sp.dma_start(rows[0:1, k * D:(k + 1) * D], v.rearrange("(o f) -> o f", o=1)).then_inc(ld_par, DMA)
                sp.dma_start(b2_row[:, :], b2.rearrange("(o f) -> o f", o=1)).then_inc(ld_par, DMA)
                sp.wait_ge(dve_pro, 4)
                sp.dma_start(rel_rows, rel_nat[:, :]).then_inc(rel_out, DMA)
                sp.wait_ge(rel_out, DMA)

            @block.gpsimd
            def _(pool):
                nc.gpsimd.iota(iota_i[:, :], pattern=[[1, W]], base=0, channel_multiplier=0).then_inc(iota_ok, 1)
                nc.gpsimd.iota(iota_pi[:, :], pattern=[[0, 1]], base=0, channel_multiplier=1).then_inc(iota_ok, 1)
                nc.gpsimd.memset(ident[:, :], 0.0).then_inc(iota_ok, 1)
                pool.wait_ge(iota_ok, 3)
                nc.gpsimd.affine_select(out=ident[:, :], in_=ident[:, :], compare_op=ALU.not_equal, fill=1.0, base=0,
                                        pattern=[[-1, P]], channel_multiplier=1).then_inc(ident_ok, 1)

            @block.vector
            def _(dve):
                nc.vector.memset(dst_nat[:, :], N - 1).then_inc(memset_ok, 1)
                nc.vector.memset(ones[:, :], 1.0)
                nc.vector.memset(eps_col[:, :], EPS)
                nc.vector.memset(no_node[:, :], NO_NODE)
                nc.vector.memset(acc_x[:, :], 0.0)
                nc.vector.memset(acc_e[:, :], 0.0)
                nc.vector.memset(acc_deg[:, :], 0.0).then_inc(memset_ok, 1)
                dve.wait_ge(iota_ok, 2)
                nc.vector.tensor_copy(iota_w[:, :], iota_i[:, :])
                nc.vector.tensor_copy(iota_p[:, :], iota_pi[:, :])
                nc.vector.tensor_scalar(floor_i[:, :], iota_pi[0:G, :], 1, None, ALU.arith_shift_right).then_inc(memset_ok, 1)
                dve.wait_ge(memset_ok, 3)
                nc.vector.tensor_scalar(floor[:, :], floor_i[:, :], float(BN), float(-BN), ALU.mult, ALU.add)
                dve.wait_ge(ld_dst, 2 * DMA)
                nc.vector.tensor_copy(dst_f[:, :], dst_nat[:, :]).then_inc(dve_pro, 1)
                dve.wait_ge(dve_pro, 1)
                nc.vector.tensor_reduce(low[:, :], dst_f[:, :], AX_X, ALU.min)
                nc.vector.tensor_reduce(high[:, :], dst_f[:, :], AX_X, ALU.max).then_inc(dve_pro, 1)
                dve.wait_ge(dve_pro, 2)
                nc.vector.tensor_scalar(base[:, :], low[:, :], float(BASE_MAX), None, ALU.min).then_inc(dve_pro, 1)
                dve.wait_ge(dve_pro, 3)
                nc.vector.tensor_scalar(rel_nat[:, :], dst_f[:, :], base[:, 0:1], None, ALU.subtract).then_inc(dve_pro, 1)
                nc.vector.tensor_scalar(base_l[:, :], ones[0:G, :], base[:, 0:1], None, ALU.mult)
                nc.vector.tensor_tensor(spread[:, :], high[:, :], base[:, :], ALU.subtract)
                nc.vector.tensor_tensor(fits[:, 1:2], low[:, :], floor[:, :], ALU.is_ge).then_inc(dve_pro, 1)
                dve.wait_ge(dve_pro, 5)
                nc.vector.tensor_scalar(fits[:, 0:1], spread[:, :], float(W - 1), None, ALU.is_le).then_inc(dve_pro, 1)
                dve.wait_ge(dve_pro, 6)
                nc.vector.tensor_tensor(ok[:, :], fits[:, 0:1], fits[:, 1:2], ALU.mult).then_inc(dve_pro, 1)
                dve.wait_ge(ident_ok, 1)
                nc.vector.tensor_copy(identb[:, :], ident[:, :])
                dve.wait_ge(pe_pro, 2)
                nc.vector.tensor_copy(base_bc[:, :], ps_agg[0][:, 0:G])
                nc.vector.tensor_copy(base_i[:, :], ps_agg[0][0:1, 0:G])
                nc.vector.tensor_copy(ok_i[:, :], ps_agg[1][0:1, 0:1])

            @block.tensor
            def _(pe):
                pe.wait_ge(ident_ok, 1)
                pe.wait_ge(memset_ok, 2)
                pe.wait_ge(ld_par, 11 * DMA)
                for k, w in enumerate((wmsg_sb, wmsg_sb, wapp_sb, wapp_sb)):
                    nc.tensor.transpose(ps4[0][:, k * D:(k + 1) * D], w[:, (k % 2) * D:(k % 2 + 1) * D], ident[:, :])
                nc.tensor.matmul(ps4[1][:, 0:3 * D], ones[0:1, :], rows[0:1, 3 * D:6 * D], start=True, stop=True)
                nc.tensor.matmul(ps4[2][:, 0:1], ones[0:1, :], b2_row[:, :], start=True, stop=True).then_inc(pe_pro, 1)
                pe.wait_ge(dve_pro, 7)
                nc.tensor.matmul(ps_agg[0][:, 0:G], base_l[:, :], ident[0:G, 0:G], start=True, stop=True)
                nc.tensor.matmul(ps_agg[1][0:1, 0:1], ok[:, :], ones[0:G, 0:1], start=True, stop=True).then_inc(pe_pro, 1)

            @block.scalar
            def _(act):
                act.wait_ge(pe_pro, 1)
                nc.scalar.copy(wT[:, :, :].rearrange("p a b -> p (a b)"), ps4[0][:, :])
                nc.scalar.copy(bcast[:, :, :].rearrange("p a b -> p (a b)"), ps4[1][:, 0:3 * D])
                nc.scalar.copy(b2_col[:, :], ps4[2][:, 0:1])

        fitting = nc.values_load(ok_i[0:1, 0:1], min_val=0, max_val=G)

        waT, wbT, wcT, wdT = (wT[:, k, :] for k in range(4))
        b_msg_row, b_app_row, b1_row = (rows[0:1, k * D:(k + 1) * D] for k in range(3))
        w2_bc, gamma_bc, beta_bc = (bcast[0:P, k, :] for k in range(3))

        def wait_apart(eng, semaphore, value):
            eng.wait_ge(semaphore, value)
            eng.sem_inc(passed, 1)

        def dve_moments(dve, done, at, v, values):
            nc.vector.bn_stats(stats[:, v, :], values).then_inc(done, 1)
            wait_apart(dve, done, at + 1)
            nc.vector.bn_aggr(moments[:, v, :], stats[:, v, :]).then_inc(done, 1)

        def act_root(act, done, at, rooted, v):
            act.wait_ge(done, at + 2)
            nc.scalar.activation(std[:, v:v + 1], moments[:, v, 1:2], ACT.Sqrt, bias=eps_col[:, 0:1]).then_inc(rooted, 1)

        def dve_normalise(dve, done, at, rooted, n, v, values, result):
            dve.wait_ge(rooted, n)
            nc.vector.reciprocal(rstd[:, v:v + 1], std[:, v:v + 1]).then_inc(done, 1)
            dve.wait_ge(done, at + 1)
            nc.vector.tensor_scalar(result, values, moments[:, v, 0:1], rstd[:, v:v + 1], ALU.subtract,
                                    ALU.mult).then_inc(done, 1)

        def sp_x_block(sp, t, v, size=BN):
            if there(t - 1):
                wait_apart(sp, ln0[v], LN0_STEPS * (t - 1) + 3)
                sp.wait_ge(prod, 2 * t + v - 1)
            sp.dma_start(x_blk[0:size, v, :], x[bass.ds(BN * (2 * t + v), size), :]).then_inc(x_in[v], DMA)

        def act_cut0(act, t, v):
            b = 2 * t + v
            if there(t - 1):
                act.wait_ge(prod, b - 1)
            for to, of, n in ((n_x, acc_x, D), (n_e, acc_e, D), (n_deg, acc_deg, 1)):
                last = nc.scalar.copy(to[0:n, v, :], of[0:n, bass.ds(BN * b, BN)])
            last.then_inc(cut, 1)

        def pe_products0(pe, t, v):
            a, c, b = ps4[2 * v], ps4[2 * v + 1], 2 * t + v
            pe.wait_ge(cut, b + 1)
            pe.wait_ge(x_in[v], DMA * (t + 1))
            if there(t - 1):
                pe.wait_ge(parts, b - 1)
                pe.wait_ge(p_cp, b - 1)
            nc.tensor.matmul(a[:, 0:BN], waT, n_x[:, v, :], start=True, stop=False)
            nc.tensor.matmul(a[:, 0:BN], wbT, n_e[:, v, :], start=False, stop=False)
            nc.tensor.matmul(a[:, 0:BN], b_msg_row, n_deg[:, v, :], start=False, stop=True)
            nc.tensor.transpose(a[:, D:D + BN], x_blk[:, v, :], ident[0:BN, 0:BN])
            nc.tensor.matmul(c[0:BN, 3 * D:3 * D + 1], n_deg[:, v, :], ones[0:1, 0:1], start=True, stop=True).then_inc(prod, 1)

        def act_products0(act, t, v):
            b = 2 * t + v
            act.wait_ge(prod, b + 1)
            if there(t - 1):
                act.wait_ge(mix, b - 1)
            nc.scalar.copy(hsT[:, v, :], ps4[2 * v][:, 0:BN])
            nc.scalar.copy(xT[:, v, :], ps4[2 * v][:, D:D + BN]).then_inc(prod_cp, 1)

        def pe_mix0(pe, t, v):
            c = ps4[2 * v + 1]
            pe.wait_ge(prod_cp, 2 * t + v + 1)
            nc.tensor.matmul(c[0:BN, 0:D], hsT[:, v, :], wdT, start=True, stop=True)
            nc.tensor.matmul(c[0:BN, D:2 * D], xT[:, v, :], wcT, start=True, stop=False)
            nc.tensor.matmul(c[0:BN, D:2 * D], ones[0:1, 0:BN], b_app_row, start=False, stop=True).then_inc(mix, 1)

        def dve_sum0(dve, t, v):
            c, b, at = ps4[2 * v + 1], 2 * t + v, LN0_STEPS * t
            dve.wait_ge(mix, b + 1)
            nc.vector.tensor_scalar(deg_max[:, v:v + 1], c[0:BN, 3 * D:3 * D + 1], 1.0, None, ALU.max).then_inc(deg_steps, 1)
            dve.wait_ge(deg_steps, 2 * b + 1)
            nc.vector.reciprocal(deg_inv[:, v:v + 1], deg_max[:, v:v + 1]).then_inc(deg_steps, 1)
            dve.wait_ge(deg_steps, 2 * b + 2)
            nc.vector.tensor_scalar(z[:, v, :], c[0:BN, 0:D], deg_inv[:, v:v + 1], None, ALU.mult).then_inc(ln0[v], 1)
            dve.wait_ge(ln0[v], at + 1)
            nc.vector.tensor_tensor(z[:, v, :], z[:, v, :], c[0:BN, D:2 * D], ALU.add).then_inc(ln0[v], 1)
            dve.wait_ge(ln0[v], at + 2)
            nc.vector.scalar_tensor_tensor(y[:, v, :], z[:, v, :], 0.0, x_blk[:, v, :], ALU.max, ALU.add).then_inc(ln0[v], 1)
            dve.wait_ge(ln0[v], at + 3)
            dve_moments(dve, ln0[v], at + 3, v, y[:, v, :])

        def act_root0(act, t, v):
            act_root(act, ln0[v], LN0_STEPS * t + 3, root0[v], v)

        def dve_norm0(dve, t, v):
            if there(t - 1):
                dve.wait_ge(tab_out[v], 2 * DMA * t)
            dve_normalise(dve, ln0[v], LN0_STEPS * t + 5, root0[v], t + 1, v, y[:, v, :], tab_blk[:, v, 0:D])

        def pe_turn0(pe, t, v):
            pe.wait_ge(ln0[v], LN0_STEPS * (t + 1))
            nc.tensor.transpose(ps4[2 * v + 1][:, 2 * D:2 * D + BN], tab_blk[:, v, 0:D], ident[0:BN, 0:BN]).then_inc(x1_tr, 1)

        def act_turn0(act, t, v):
            b = 2 * t + v
            act.wait_ge(x1_tr, b + 1)
            if there(t - 1):
                act.wait_ge(pq, b - 1)
            nc.scalar.copy(x1T[:, v, :], ps4[2 * v + 1][:, 2 * D:2 * D + BN]).then_inc(x1_cp, 1)

        def pe_pq0(pe, t, v):
            a, c = ps4[2 * v], ps4[2 * v + 1]
            pe.wait_ge(x1_cp, 2 * t + v + 1)
            nc.tensor.matmul(c[0:BN, 0:D], x1T[:, v, :], w1_sb[:, 0:D], start=True, stop=False)
            nc.tensor.matmul(c[0:BN, 0:D], ones[0:1, 0:BN], b1_row, start=False, stop=True)
            nc.tensor.matmul(a[0:BN, 3 * D:4 * D], x1T[:, v, :], w1_sb[:, D:2 * D], start=True, stop=True).then_inc(pq, 1)

        def dve_parts0(dve, t, v):
            q, b = ps4[2 * v][0:BN, 3 * D:4 * D], 2 * t + v
            hi, mid, lo = (q_blk[:, v, k * D:(k + 1) * D] for k in range(3))
            dve.wait_ge(pq, b + 1)
            if there(t - 1):
                dve.wait_ge(tab_out[v], 2 * DMA * t)
            nc.vector.tensor_copy(hi, q).then_inc(q_split, 1)
            dve.wait_ge(q_split, 3 * b + 1)
            nc.vector.tensor_tensor(q_rest[:, v, 0, :], q, hi, ALU.subtract).then_inc(q_split, 1)
            dve.wait_ge(q_split, 3 * b + 2)
            nc.vector.tensor_copy(mid, q_rest[:, v, 0, :]).then_inc(q_split, 1)
            dve.wait_ge(q_split, 3 * b + 3)
            nc.vector.tensor_tensor(lo, q_rest[:, v, 0, :], mid, ALU.subtract).then_inc(parts, 1)

        def act_store0(act, t, v):
            b = 2 * t + v
            act.wait_ge(pq, b + 1)
            if there(t - 1):
                act.wait_ge(tab_out[v], 2 * DMA * t)
            nc.scalar.copy(tab_blk[:, v, D:2 * D], ps4[2 * v + 1][0:BN, 0:D]).then_inc(p_cp, 1)
            act.wait_ge(p_cp, b + 1)
            act.dma_start(table[bass.ds(BN * b, BN), :], tab_blk[:, v, :]).then_inc(tab_out[v], DMA)
            act.wait_ge(parts, b + 1)
            act.dma_start(q_parts[bass.ds(BN * b, BN), :], q_blk[:, v, :]).then_inc(tab_out[v], DMA)

        def sp_x1_block(sp, t, v):
            if there(t - 1):
                sp.wait_ge(ln1[v], LN1_STEPS * (t - 1) + 8)
            sp.dma_start(x_blk[:, v, :], table[bass.ds(BN * (2 * t + v), BN), 0:D]).then_inc(x1_in[v], DMA)

        def act_cut1(act, t, v):
            b = 2 * t + v
            if there(t - 1):
                act.wait_ge(sum_tr, b - 1)
            nc.scalar.copy(n_x[:, v, :], acc_x[:, bass.ds(BN * b, BN)]).then_inc(cut1, 1)

        def pe_turn1(pe, t, v):
            pe.wait_ge(cut1, 2 * t + v + 1)
            if there(t - 1):
                pe.wait_ge(ln1[v], LN1_STEPS * (t - 1) + 1)
            nc.tensor.transpose(ps_fin[v][0:BN, 0:D], n_x[:, v, :], ident[:, :]).then_inc(sum_tr, 1)

        def dve_first1(dve, t, v):
            at = LN1_STEPS * t
            dve.wait_ge(sum_tr, 2 * t + v + 1)
            dve.wait_ge(x1_in[v], DMA * (t + 1))
            nc.vector.tensor_tensor(z[:, v, :], ps_fin[v][0:BN, 0:D], x_blk[:, v, :], ALU.add).then_inc(ln1[v], 1)
            dve.wait_ge(ln1[v], at + 1)
            dve_moments(dve, ln1[v], at + 1, v, z[:, v, :])

        def dve_second1(dve, t, v):
            at = LN1_STEPS * t
            dve_normalise(dve, ln1[v], at + 3, root1[v], 2 * t + 1, v, z[:, v, :], y[:, v, :])
            dve.wait_ge(ln1[v], at + 5)
            nc.vector.tensor_tensor(z[:, v, :], y[:, v, :], gamma_bc[0:BN, :], ALU.mult).then_inc(ln1[v], 1)
            dve.wait_ge(ln1[v], at + 6)
            nc.vector.tensor_tensor(y[:, v, :], z[:, v, :], beta_bc[0:BN, :], ALU.add).then_inc(ln1[v], 1)
            dve.wait_ge(ln1[v], at + 7)
            nc.vector.tensor_tensor(z[:, v, :], y[:, v, :], x_blk[:, v, :], ALU.add).then_inc(ln1[v], 1)
            dve.wait_ge(ln1[v], at + 8)
            dve_moments(dve, ln1[v], at + 8, v, z[:, v, :])

        def dve_third1(dve, t, v):
            if there(t - 1):
                dve.wait_ge(fin_out[v], DMA * t)
            dve_normalise(dve, ln1[v], LN1_STEPS * t + 10, root1[v], 2 * t + 2, v, z[:, v, :], fin[:, v, :])

        def act_root1(act, t, v, second):
            act_root(act, ln1[v], LN1_STEPS * t + (8 if second else 1), root1[v], v)

        def act_store1(act, t, v, size=BN):
            act.wait_ge(ln1[v], LN1_STEPS * (t + 1))
            act.dma_start(out[bass.ds(BN * (2 * t + v), size), :], fin[0:size, v, :]).then_inc(fin_out[v], DMA)

        def accumulate(dve, psum_cols, into, at):
            return nc.vector.tensor_tensor(into[:, bass.ds(at, W)], into[:, bass.ds(at, W)], psum_cols, ALU.add)

        def tables_stored(eng):
            for v in range(2):
                eng.wait_ge(tab_out[v], NB * DMA)

        def dve_logits(dve, u, g, first_bank):
            dve.wait_ge(h_done, g + 1)
            for j in range(TILES):
                cols = ps4[first_bank + j // 4][:, (j % 4) * D:(j % 4 + 1) * D]
                last = nc.vector.scalar_tensor_tensor(act_out[:, j, :], cols, 0.0, w2_bc, ALU.max, ALU.mult,
                                                      accum_out=logit[:, u, j:j + 1])
            last.then_inc(dot_done, 1)

        def act_weights(act, u, g):
            act.wait_ge(dot_done, g + 1)
            nc.scalar.activation(weight[:, u, :], logit[:, u, :], ACT.Sigmoid, bias=b2_col[:, 0:1]).then_inc(sig_done, 1)

        def windowed():
            with nc.Block() as block:
                @block.sync
                def _(sp):
                    def load(i, u, last=False):
                        g = SLOTS * i + u
                        if there(i - 1):
                            sp.wait_ge(gath0[u], TILES * DMA * i)
                        if last:
                            sp.dma_start(src_slot[0:REST_P, u, :], src_rest).then_inc(src_in0[u], DMA)
                            sp.dma_start(src_slot[REST_P:REST_P + 1, u, 0:REST_J], src_end).then_inc(src_in0[u], DMA)
                        else:
                            sp.dma_start(src_slot[:, u, :], src_g[g]).then_inc(src_in0[u], DMA)
                        if there(i - 1):
                            sp.wait_ge(rel_done, g - SLOTS + 1)
                        if last:
                            sp.dma_start(dst_slot[:, u, :], no_node[:, :]).then_inc(pad_in, DMA)
                            sp.wait_ge(pad_in, DMA)
                            sp.dma_start(dst_slot[0:REST_P, u, :], dst_rest).then_inc(dst_in[u], DMA)
                            sp.dma_start(dst_slot[REST_P:REST_P + 1, u, 0:REST_J], dst_end).then_inc(dst_in[u], DMA)
                        else:
                            sp.dma_start(dst_slot[:, u, :], dst_g[g]).then_inc(dst_in[u], DMA)
                        if there(i - 1):
                            sp.wait_ge(agg0, g - SLOTS + 1)
                        if last:
                            sp.dma_start(ring[0:REST_P, u, GE:2 * GE], edge_rest).then_inc(edge_in[u], DMA)
                            sp.dma_start(ring[REST_P:REST_P + 1, u, GE:GE + REST_J * D], edge_end).then_inc(edge_in[u], DMA)
                        else:
                            sp.dma_start(ring[:, u, GE:2 * GE], edge_g[g]).then_inc(edge_in[u], DMA)
                        block = block_back(i, u, 1)
                        if u % 2 == 1 and there(block[0]):
                            sp_x_block(sp, *block)

                    for n in range(PEELED * SLOTS):
                        load(*divmod(n, SLOTS))
                    with sp.Fori(PEELED, TURNS - 1) as i:
                        for u in range(SLOTS):
                            load(i, u)
                    for u in range(SLOTS):
                        load(TURNS - 1, u, last=u == SLOTS - 1)
                    sp_x_block(sp, NB // 2 - 1, 1, LAST_BN)

                @block.gpsimd
                def _(pool):
                    def gather(i, u):
                        g = SLOTS * i + u
                        pool.wait_ge(src_in0[u], DMA * (i + 1 + is_last(i, u)))
                        if there(i - 1):
                            wait_apart(pool, agg0, g - SLOTS + 1)
                        for j in range(TILES):
                            nc.gpsimd.indirect_dma_start(
                                out=ring[:, u, j * D:(j + 1) * D], out_offset=None, in_=x,
                                in_offset=bass.IndirectOffsetOnAxis(ap=src_slot[:, u, j:j + 1], axis=0),
                            ).then_inc(gath0[u], DMA)

                    for n in range(PEELED * SLOTS):
                        gather(*divmod(n, SLOTS))
                    with pool.Fori(PEELED, TURNS - 1) as i:
                        for u in range(SLOTS):
                            gather(i, u)
                    for u in range(SLOTS):
                        gather(TURNS - 1, u)

                @block.vector
                def _(dve):
                    def sums(i, u):
                        g = SLOTS * i + u
                        at = dve.value_load(base_i[0:1, bass.ds(g, 1)], min_val=0, max_val=BASE_MAX)
                        dve.wait_ge(agg0, g + 1)
                        if there(g - 1):
                            dve.wait_ge(acc0, g)
                        ps = ps_agg[u % 2]
                        accumulate(dve, ps[:, 0:W], acc_x, at)
                        accumulate(dve, ps[:, W:2 * W], acc_e, at)
                        accumulate(dve, ps[0:1, 2 * W:3 * W], acc_deg, at).then_inc(acc0, 1)

                    def one_hots(i, u):
                        g = SLOTS * i + u
                        dve.wait_ge(dst_in[u], DMA * (i + 1 + is_last(i, u)))
                        nc.vector.tensor_scalar(rel[:, bass.ds(TILES * g, TILES)], dst_slot[:, u, :],
                                                base_bc[:, bass.ds(g, 1)], None, ALU.subtract).then_inc(rel_done, 1)
                        dve.wait_ge(rel_done, g + 1)
                        if there(i - 1):
                            dve.wait_ge(agg0, g - SLOTS + 1)
                        for j in range(TILES):
                            last = nc.vector.tensor_scalar(S[:, u, j, :], iota_w[:, :],
                                                           rel[:, bass.ds(TILES * g + j, 1)], None, ALU.is_equal)
                        last.then_inc(s_ready, 1)
                        dve.wait_ge(s_ready, g + 1)
                        nc.vector.tensor_reduce(S_sum[:, u, :], S[:, u, :, :].rearrange("p j w -> p w j"), AX_X,
                                                ALU.add).then_inc(sum_ready, 1)

                    def step(i, u):
                        if not is_last(i, u):
                            one_hots(*ahead(i, u))
                        before, block, block_before = back(i, u, 1), block_back(i, u, 2), block_back(i, u, 3)
                        if u % 2 == 1 and there(block[0]):
                            dve_sum0(dve, *block)
                        if there(before[0]):
                            sums(*before)
                        if u % 2 == 1 and there(block[0]):
                            dve_norm0(dve, *block)
                        if u % 2 == 0 and there(block_before[0]):
                            dve_parts0(dve, *block_before)

                    one_hots(0, 0)
                    for n in range(PEELED * SLOTS):
                        step(*divmod(n, SLOTS))
                    with dve.Fori(PEELED, TURNS - 1) as i:
                        for u in range(SLOTS):
                            step(i, u)
                    for u in range(SLOTS):
                        step(TURNS - 1, u)
                    sums(TURNS - 1, SLOTS - 1)
                    dve_parts0(dve, NB // 2 - 2, 1)
                    for phase in (dve_sum0, dve_norm0, dve_parts0):
                        for v in range(2):
                            phase(dve, NB // 2 - 1, v)
                    dve.wait_ge(cut, NB)
                    nc.vector.memset(acc_x[:, :], 0.0).then_inc(cleared, 1)

                @block.tensor
                def _(pe):
                    def summed(u, at, lhs_at):
                        for j in range(TILES):
                            nc.tensor.matmul(ps_agg[u % 2][:, at:at + W],
                                             ring[:, u, lhs_at + j * D:lhs_at + (j + 1) * D], S[:, u, j, :],
                                             start=j == 0, stop=j == TILES - 1)

                    def step(i, u):
                        g = SLOTS * i + u
                        block, block_before = block_back(i, u, 2), block_back(i, u, 3)
                        pe.wait_ge(gath0[u], TILES * DMA * (i + 1))
                        pe.wait_ge(s_ready, g + 1)
                        if there(g - 2):
                            pe.wait_ge(acc0, g - 1)
                        summed(u, 0, 0)
                        if u % 2 == 0 and there(block_before[0]):
                            pe_pq0(pe, *block_before)
                        if u % 2 == 0 and there(block[0]):
                            pe_products0(pe, *block)
                        pe.wait_ge(edge_in[u], DMA * (i + 1 + is_last(i, u)))
                        summed(u, W, GE)
                        pe.wait_ge(sum_ready, g + 1)
                        nc.tensor.matmul(ps_agg[u % 2][0:1, 2 * W:3 * W], ones[:, 0:1], S_sum[:, u, :], start=True,
                                         stop=True).then_inc(agg0, 1)
                        if u % 2 == 0 and there(block[0]):
                            pe_mix0(pe, *block)
                        if u % 2 == 1 and there(block[0]):
                            pe_turn0(pe, *block)

                    for n in range(PEELED * SLOTS):
                        step(*divmod(n, SLOTS))
                    with pe.Fori(PEELED, TURNS - 1) as i:
                        for u in range(SLOTS):
                            step(i, u)
                    for u in range(SLOTS):
                        step(TURNS - 1, u)
                    pe_pq0(pe, NB // 2 - 2, 1)
                    for phase in (pe_products0, pe_mix0, pe_turn0, pe_pq0):
                        for v in range(2):
                            phase(pe, NB // 2 - 1, v)

                @block.scalar
                def _(act):
                    def step(i, u):
                        block, block_before = block_back(i, u, 2), block_back(i, u, 3)
                        if u % 2 == 0 and there(block[0]):
                            act.wait_ge(acc0, SLOTS * i + u)
                            act_cut0(act, *block)
                            act_products0(act, *block)
                        if u % 2 == 0 and there(block_before[0]):
                            act_store0(act, *block_before)
                        if u % 2 == 1 and there(block[0]):
                            act_root0(act, *block)
                            act_turn0(act, *block)

                    for n in range(PEELED * SLOTS):
                        step(*divmod(n, SLOTS))
                    with act.Fori(PEELED, TURNS) as i:
                        for u in range(SLOTS):
                            step(i, u)
                    act_store0(act, NB // 2 - 2, 1)
                    act.wait_ge(acc0, G)
                    for phase in (act_cut0, act_products0, act_root0, act_turn0, act_store0):
                        for v in range(2):
                            phase(act, NB // 2 - 1, v)
                    tables_stored(act)

            with nc.Block() as block:
                @block.sync
                def _(sp):
                    def load(i, u, last=False):
                        g = SLOTS * i + u
                        if there(i - 1):
                            sp.wait_ge(gath1[u], TILES * DMA * i)
                        if last:
                            sp.dma_start(src_slot[0:REST_P, u, :], src_rest).then_inc(src_in1[u], DMA)
                            sp.dma_start(src_slot[REST_P:REST_P + 1, u, 0:REST_J], src_end).then_inc(src_in1[u], DMA)
                        else:
                            sp.dma_start(src_slot[:, u, :], src_g[g]).then_inc(src_in1[u], DMA)
                        if there(i - 1):
                            wait_apart(sp, st_ready, g - SLOTS + 1)
                        sp.dma_start(rel_bc[:, u, :], rel_rows[bass.ds(g, 1), :].to_broadcast([P, GE])).then_inc(row_in[u], DMA)
                        at = sp.value_load(base_i[0:1, bass.ds(g, 1)], min_val=0, max_val=BASE_MAX)
                        if there(i - 1):
                            sp.wait_ge(h_done, g - SLOTS + 1)
                        sp.dma_start(q_win[:, u, :], q_parts[bass.ds(at, W), :]).then_inc(q_in[u], DMA)
                        block = block_back(i, u, 2)
                        if u % 2 == 1 and there(block[0]):
                            sp_x1_block(sp, *block)

                    for n in range(PEELED * SLOTS):
                        load(*divmod(n, SLOTS))
                    with sp.Fori(PEELED, TURNS - 1) as i:
                        for u in range(SLOTS):
                            load(i, u)
                    for u in range(SLOTS):
                        load(TURNS - 1, u, last=u == SLOTS - 1)
                    for v in range(2):
                        sp_x1_block(sp, NB // 2 - 1, v)

                @block.gpsimd
                def _(pool):
                    def gather(i, u):
                        g = SLOTS * i + u
                        pool.wait_ge(src_in1[u], DMA * (i + 1 + is_last(i, u)))
                        if there(i - 1):
                            wait_apart(pool, agg1, g - SLOTS + 1)
                        for j in range(TILES):
                            nc.gpsimd.indirect_dma_start(
                                out=ring[:, u, 2 * j * D:2 * (j + 1) * D], out_offset=None, in_=table,
                                in_offset=bass.IndirectOffsetOnAxis(ap=src_slot[:, u, j:j + 1], axis=0),
                            ).then_inc(gath1[u], DMA)

                    for n in range(PEELED * SLOTS):
                        gather(*divmod(n, SLOTS))
                    with pool.Fori(PEELED, TURNS - 1) as i:
                        for u in range(SLOTS):
                            gather(i, u)
                    for u in range(SLOTS):
                        gather(TURNS - 1, u)

                @block.vector
                def _(dve):
                    def sums(i, u):
                        g = SLOTS * i + u
                        at = dve.value_load(base_i[0:1, bass.ds(g, 1)], min_val=0, max_val=BASE_MAX)
                        dve.wait_ge(agg1, g + 1)
                        if there(g - 1):
                            dve.wait_ge(acc1, g)
                        accumulate(dve, ps_agg[u % 2][:, 0:W], acc_x, at).then_inc(acc1, 1)

                    def one_hots(i, u):
                        g = SLOTS * i + u
                        dve.wait_ge(row_in[u], DMA * (i + 1))
                        if there(i - 1):
                            dve.wait_ge(h_done, g - SLOTS + 1)
                        nc.vector.tensor_scalar(ST[:, u, :, :].rearrange("w j p -> w p j"),
                                                rel_bc[:, u, :].rearrange("w (p j) -> w p j", j=TILES),
                                                iota_p[:, 0:1], None, ALU.is_equal).then_inc(st_ready, 1)

                    def step(i, u):
                        if not is_last(i, u):
                            one_hots(*ahead(i, u))
                        before, two_before = back(i, u, 1), back(i, u, 2)
                        block, block_before = block_back(i, u, 3), block_back(i, u, 4)
                        if there(before[0]):
                            dve_logits(dve, before[1], SLOTS * before[0] + before[1], 2 * (before[1] % 2))
                        if there(two_before[0]):
                            sums(*two_before)
                        if there(before[0]):
                            weigh(*before)
                        if u % 2 == 0 and there(block_before[0]):
                            dve_third1(dve, *block_before)
                        if u % 2 == 0 and there(block[0]):
                            dve_first1(dve, *block)
                        if u % 2 == 1 and there(block[0]):
                            dve_second1(dve, *block)

                    def weigh(i, u):
                        g = SLOTS * i + u
                        dve.wait_ge(sig_done, g + 1)
                        if there(i - 1):
                            dve.wait_ge(agg1, g - SLOTS + 1)
                        for j in range(TILES):
                            last = nc.vector.tensor_scalar(S[:, u, j, :], iota_w[:, :], rel[:, bass.ds(TILES * g + j, 1)],
                                                           weight[:, u, j:j + 1], ALU.is_equal, ALU.mult)
                        last.then_inc(sw_ready, 1)

                    dve.wait_ge(cleared, 1)
                    one_hots(0, 0)
                    for n in range(PEELED * SLOTS):
                        step(*divmod(n, SLOTS))
                    with dve.Fori(PEELED, TURNS - 1) as i:
                        for u in range(SLOTS):
                            step(i, u)
                    for u in range(SLOTS):
                        step(TURNS - 1, u)
                    dve_logits(dve, SLOTS - 1, G - 1, 2)
                    sums(TURNS - 1, SLOTS - 2)
                    weigh(TURNS - 1, SLOTS - 1)
                    pair = NB // 2 - 1
                    dve_third1(dve, pair - 1, 0)
                    dve_first1(dve, pair - 1, 1)
                    dve_second1(dve, pair - 1, 1)
                    sums(TURNS - 1, SLOTS - 1)
                    dve_third1(dve, pair - 1, 1)
                    for phase in (dve_first1, dve_second1, dve_third1):
                        for v in range(2):
                            phase(dve, pair, v)

                @block.tensor
                def _(pe):
                    def pre_activation(i, u):
                        g = SLOTS * i + u
                        pe.wait_ge(gath1[u], TILES * DMA * (i + 1))
                        pe.wait_ge(q_in[u], DMA * (i + 1))
                        pe.wait_ge(st_ready, g + 1)
                        if there(g - 2):
                            pe.wait_ge(dot_done, g - 1)
                        for j in range(TILES):
                            cols = ps4[2 * (u % 2) + j // 4][:, (j % 4) * D:(j % 4 + 1) * D]
                            nc.tensor.matmul(cols, ident[:, :], ring[:, u, (2 * j + 1) * D:(2 * j + 2) * D], start=True, stop=False)
                            for k in range(3):
                                last = nc.tensor.matmul(cols, ST[:, u, j, :], q_win[:, u, k * D:(k + 1) * D],
                                                        start=False, stop=k == 2)
                        last.then_inc(h_done, 1)

                    def summed(i, u):
                        g = SLOTS * i + u
                        pe.wait_ge(sw_ready, g + 1)
                        if there(g - 2):
                            pe.wait_ge(acc1, g - 1)
                        for j in range(TILES):
                            last = nc.tensor.matmul(ps_agg[u % 2][:, 0:W], ring[:, u, 2 * j * D:(2 * j + 1) * D],
                                                    S[:, u, j, :], start=j == 0, stop=j == TILES - 1)
                        last.then_inc(agg1, 1)

                    def step(i, u):
                        block = block_back(i, u, 3)
                        pre_activation(i, u)
                        if u % 2 == 0 and there(block[0]):
                            pe_turn1(pe, *block)
                        before = back(i, u, 1)
                        if there(before[0]):
                            summed(*before)

                    for n in range(PEELED * SLOTS):
                        step(*divmod(n, SLOTS))
                    with pe.Fori(PEELED, TURNS) as i:
                        for u in range(SLOTS):
                            step(i, u)
                    pe_turn1(pe, NB // 2 - 2, 1)
                    summed(TURNS - 1, SLOTS - 1)
                    for v in range(2):
                        pe_turn1(pe, NB // 2 - 1, v)

                @block.scalar
                def _(act):
                    def step(i, u):
                        before, block, block_before = back(i, u, 1), block_back(i, u, 3), block_back(i, u, 4)
                        if u % 2 == 0 and there(block[0]):
                            act.wait_ge(acc1, SLOTS * i + u - 2)
                            act_cut1(act, *block)
                        if there(before[0]):
                            act_weights(act, before[1], SLOTS * before[0] + before[1])
                        if u % 2 == 0 and there(block_before[0]):
                            act_store1(act, *block_before)
                        if there(block[0]):
                            act_root1(act, *block, u % 2 == 1)

                    for n in range(PEELED * SLOTS):
                        step(*divmod(n, SLOTS))
                    with act.Fori(PEELED, TURNS) as i:
                        for u in range(SLOTS):
                            step(i, u)
                    pair = NB // 2 - 1
                    act_cut1(act, pair - 1, 1)
                    act_weights(act, SLOTS - 1, G - 1)
                    act_store1(act, pair - 1, 0)
                    act_root1(act, pair - 1, 1, False)
                    act_root1(act, pair - 1, 1, True)
                    act.wait_ge(acc1, G)
                    for v in range(2):
                        act_cut1(act, pair, v)
                    act_store1(act, pair - 1, 1)
                    for second in (False, True):
                        for v in range(2):
                            act_root1(act, pair, v, second)
                    act_store1(act, pair, 0)
                    act_store1(act, pair, 1, LAST_BN)
                    for v in range(2):
                        act.wait_ge(fin_out[v], DMA * NB // 2)

        def general():
            def groups(eng, step):
                with eng.Fori(0, G - 1) as g:
                    step(g, False)
                step(G - 1, True)

            def blocks(eng, *phases):
                def pair(t):
                    for v in range(2):
                        for phase in phases:
                            phase(eng, t, v)

                pair(0)
                with eng.Fori(1, NB // 2 - 1) as t:
                    pair(t)
                pair(NB // 2 - 1)

            def size_of(t, v):
                return LAST_BN if isinstance(t, int) and 2 * t + v == NB - 1 else BN

            def load_indices(sp, g, last, acc, src_in):
                sp.wait_ge(acc, WINDOWS * g + 1)
                if last:
                    sp.dma_start(src_slot[0:REST_P, 0, :], src_rest).then_inc(src_in, DMA)
                    sp.dma_start(src_slot[REST_P:REST_P + 1, 0, 0:REST_J], src_end).then_inc(src_in, DMA)
                    sp.dma_start(dst_slot[:, 0, :], no_node[:, :]).then_inc(pad_in, DMA)
                    sp.wait_ge(pad_in, DMA if acc is acc0 else 2 * DMA)
                    sp.dma_start(dst_slot[0:REST_P, 0, :], dst_rest).then_inc(dst_in[0], DMA)
                    sp.dma_start(dst_slot[REST_P:REST_P + 1, 0, 0:REST_J], dst_end).then_inc(dst_in[0], DMA)
                else:
                    sp.dma_start(src_slot[:, 0, :], src_g[g]).then_inc(src_in, DMA)
                    sp.dma_start(dst_slot[:, 0, :], dst_g[g]).then_inc(dst_in[0], DMA)

            def start_windows(dve, g, last, groups_before):
                dve.wait_ge(dst_in[0], DMA * (groups_before + g + 1 + last))
                nc.vector.tensor_scalar(rel[:, 0:TILES], dst_slot[:, 0, :], float(W), None, ALU.add).then_inc(rel_done, 1)

            def next_window(dve, n):
                dve.wait_ge(rel_done, n)
                nc.vector.tensor_scalar(rel[:, 0:TILES], rel[:, 0:TILES], float(-W), None, ALU.add).then_inc(rel_done, 1)
                dve.wait_ge(rel_done, n + 1)

            REL_STEPS = WINDOWS + 1
            L1_REL = G * REL_STEPS

            with nc.Block() as block:
                @block.sync
                def _(sp):
                    def step(g, last):
                        load_indices(sp, g, last, acc0, src_in0[0])
                        if last:
                            sp.dma_start(ring[0:REST_P, 0, GE:2 * GE], edge_rest).then_inc(edge_in[0], DMA)
                            sp.dma_start(ring[REST_P:REST_P + 1, 0, GE:GE + REST_J * D], edge_end).then_inc(edge_in[0], DMA)
                        else:
                            sp.dma_start(ring[:, 0, GE:2 * GE], edge_g[g]).then_inc(edge_in[0], DMA)

                    groups(sp, step)

                @block.gpsimd
                def _(pool):
                    def step(g, last):
                        wait_apart(pool, src_in0[0], DMA * (g + 1 + last))
                        wait_apart(pool, acc0, WINDOWS * g + 1)
                        for j in range(TILES):
                            nc.gpsimd.indirect_dma_start(
                                out=ring[:, 0, j * D:(j + 1) * D], out_offset=None, in_=x,
                                in_offset=bass.IndirectOffsetOnAxis(ap=src_slot[:, 0, j:j + 1], axis=0),
                            ).then_inc(gath0[0], DMA)

                    groups(pool, step)

                @block.vector
                def _(dve):
                    def step(g, last):
                        start_windows(dve, g, last, 0)
                        with dve.Fori(0, WINDOWS) as k:
                            n = WINDOWS * g + k
                            next_window(dve, REL_STEPS * g + k + 1)
                            for j in range(TILES):
                                done = nc.vector.tensor_scalar(S[:, 0, j, :], iota_w[:, :], rel[:, j:j + 1], None, ALU.is_equal)
                            done.then_inc(s_ready, 1)
                            dve.wait_ge(s_ready, n + 1)
                            nc.vector.tensor_reduce(S_sum[:, 0, :], S[:, 0, :, :].rearrange("p j w -> p w j"), AX_X,
                                                    ALU.add).then_inc(sum_ready, 1)
                            dve.wait_ge(agg0, n + 1)
                            dve.wait_ge(acc0, n + 1)
                            accumulate(dve, ps_agg[0][:, 0:W], acc_x, W * k)
                            accumulate(dve, ps_agg[0][:, W:2 * W], acc_e, W * k)
                            accumulate(dve, ps_agg[0][0:1, 2 * W:3 * W], acc_deg, W * k).then_inc(acc0, 1)

                    nc.vector.memset(acc_x[:, :], 0.0).then_inc(acc0, 1)
                    groups(dve, step)

                @block.tensor
                def _(pe):
                    def step(g, last):
                        pe.wait_ge(gath0[0], TILES * DMA * (g + 1))
                        wait_apart(pe, edge_in[0], DMA * (g + 1 + last))
                        with pe.Fori(0, WINDOWS) as k:
                            n = WINDOWS * g + k
                            pe.wait_ge(s_ready, n + 1)
                            pe.wait_ge(acc0, n + 1)
                            for at, lhs_at in ((0, 0), (W, GE)):
                                for j in range(TILES):
                                    nc.tensor.matmul(ps_agg[0][:, at:at + W], ring[:, 0, lhs_at + j * D:lhs_at + (j + 1) * D],
                                                     S[:, 0, j, :], start=j == 0, stop=j == TILES - 1)
                            pe.wait_ge(sum_ready, n + 1)
                            nc.tensor.matmul(ps_agg[0][0:1, 2 * W:3 * W], ones[:, 0:1], S_sum[:, 0, :], start=True,
                                             stop=True).then_inc(agg0, 1)

                    groups(pe, step)

            with nc.Block() as block:
                @block.sync
                def _(sp):
                    blocks(sp, lambda sp, t, v: sp_x_block(sp, t, v, size_of(t, v)))

                @block.vector
                def _(dve):
                    blocks(dve, dve_sum0, dve_norm0, dve_parts0)

                @block.tensor
                def _(pe):
                    blocks(pe, pe_products0, pe_mix0, pe_turn0, pe_pq0)

                @block.scalar
                def _(act):
                    act.wait_ge(acc0, WINDOWS * G + 1)
                    blocks(act, act_cut0, act_products0, act_root0, act_turn0, act_store0)
                    tables_stored(act)

            with nc.Block() as block:
                @block.sync
                def _(sp):
                    def step(g, last):
                        load_indices(sp, g, last, acc1, src_in1[0])
                        if last:
                            sp.dma_start(dst_slot[0:REST_P, 1, :], dst_rest).then_inc(row_in[0], DMA)
                            sp.dma_start(dst_slot[REST_P:REST_P + 1, 1, 0:REST_J], dst_end).then_inc(row_in[0], DMA)
                        else:
                            sp.dma_start(dst_slot[:, 1, :], dst_g[g]).then_inc(row_in[0], DMA)

                    groups(sp, step)

                @block.gpsimd
                def _(pool):
                    def step(g, last):
                        wait_apart(pool, src_in1[0], DMA * (g + 1 + last))
                        wait_apart(pool, row_in[0], DMA * (g + 1 + last))
                        wait_apart(pool, acc1, WINDOWS * g + 1)
                        for j in range(TILES):
                            nc.gpsimd.indirect_dma_start(
                                out=ring[:, 0, 2 * j * D:2 * (j + 1) * D], out_offset=None, in_=table,
                                in_offset=bass.IndirectOffsetOnAxis(ap=src_slot[:, 0, j:j + 1], axis=0),
                            ).then_inc(gath1[0], DMA)
                            nc.gpsimd.indirect_dma_start(
                                out=q_rows[:, 3 * j * D:3 * (j + 1) * D], out_offset=None, in_=q_parts,
                                in_offset=bass.IndirectOffsetOnAxis(ap=dst_slot[:, 1, j:j + 1], axis=0),
                            ).then_inc(gath1[1], DMA)

                    groups(pool, step)

                @block.vector
                def _(dve):
                    def step(g, last):
                        start_windows(dve, g, last, G + 1)
                        dve_logits(dve, 0, g, 0)
                        wait_apart(dve, sig_done, g + 1)
                        with dve.Fori(0, WINDOWS) as k:
                            n = WINDOWS * g + k
                            next_window(dve, REL_STEPS * g + k + L1_REL + 1)
                            for j in range(TILES):
                                done = nc.vector.tensor_scalar(S[:, 0, j, :], iota_w[:, :], rel[:, j:j + 1],
                                                               weight[:, 0, j:j + 1], ALU.is_equal, ALU.mult)
                            done.then_inc(sw_ready, 1)
                            dve.wait_ge(agg1, n + 1)
                            dve.wait_ge(acc1, n + 1)
                            accumulate(dve, ps_agg[0][:, 0:W], acc_x, W * k).then_inc(acc1, 1)

                    nc.vector.memset(acc_x[:, :], 0.0).then_inc(acc1, 1)
                    groups(dve, step)

                @block.tensor
                def _(pe):
                    def step(g, last):
                        pe.wait_ge(gath1[0], TILES * DMA * (g + 1))
                        pe.wait_ge(gath1[1], TILES * DMA * (g + 1))
                        pe.wait_ge(acc1, WINDOWS * g + 1)
                        for j in range(TILES):
                            cols = ps4[j // 4][:, (j % 4) * D:(j % 4 + 1) * D]
                            nc.tensor.matmul(cols, ident[:, :], ring[:, 0, (2 * j + 1) * D:(2 * j + 2) * D], start=True, stop=False)
                            for k in range(3):
                                done = nc.tensor.matmul(cols, identb[:, :], q_rows[:, (3 * j + k) * D:(3 * j + k + 1) * D],
                                                        start=False, stop=k == 2)
                        done.then_inc(h_done, 1)
                        with pe.Fori(0, WINDOWS) as k:
                            n = WINDOWS * g + k
                            pe.wait_ge(sw_ready, n + 1)
                            pe.wait_ge(acc1, n + 1)
                            for j in range(TILES):
                                done = nc.tensor.matmul(ps_agg[0][:, 0:W], ring[:, 0, 2 * j * D:(2 * j + 1) * D], S[:, 0, j, :],
                                                        start=j == 0, stop=j == TILES - 1)
                            done.then_inc(agg1, 1)

                    groups(pe, step)

                @block.scalar
                def _(act):
                    groups(act, lambda g, last: act_weights(act, 0, g))

            with nc.Block() as block:
                @block.sync
                def _(sp):
                    blocks(sp, sp_x1_block)

                @block.vector
                def _(dve):
                    blocks(dve, dve_first1, dve_second1, dve_third1)

                @block.tensor
                def _(pe):
                    blocks(pe, pe_turn1)

                @block.scalar
                def _(act):
                    act.wait_ge(acc1, WINDOWS * G + 1)
                    blocks(act, act_cut1, lambda act, t, v: act_root1(act, t, v, False),
                           lambda act, t, v: act_root1(act, t, v, True),
                           lambda act, t, v: act_store1(act, t, v, size_of(t, v)))
                    for v in range(2):
                        act.wait_ge(fin_out[v], DMA * NB // 2)

        with nc.If(fitting == G):
            windowed()
        with nc.Else():
            general()


_INS = ['x', 'src', 'dst', 'edge_attr_128', 'L0_gnn_W_msg_w', 'L0_gnn_W_msg_b', 'L0_gnn_W_app_w', 'L0_gnn_W_app_b',
        'L1_gnn_W1', 'L1_gnn_b1', 'L1_gnn_W2', 'L1_gnn_b2', 'L1_gnn_gamma', 'L1_gnn_beta']


def kernel(**inputs):
    import numpy as _np
    import concourse.bacc as _bacc
    from concourse import mybir as _mybir
    from concourse.bass_utils import run_bass_kernel_spmd as _run

    nc = _bacc.Bacc("TRN2", target_bir_lowering=False, num_devices=1)
    arrays, args = {}, []
    for name in _INS:
        a = _np.ascontiguousarray(inputs[name])
        arrays[f"in_{name}_dram"] = a
        args.append(nc.dram_tensor(f"in_{name}_dram", a.shape, _mybir.dt.from_np(a.dtype), kind="ExternalInput").ap())
    args.append(nc.dram_tensor("out_0_dram", (N, D), F32, kind="ExternalOutput").ap())
    build(nc, *args)
    r = _run(nc, [arrays], core_ids=[0])
    return r.results[0]["out_0_dram"]
```

```python
import concourse.bass as bass
from concourse import mybir
from contextlib import ExitStack

F32 = mybir.dt.float32
BF16 = mybir.dt.bfloat16
I32 = mybir.dt.int32
ALU = mybir.AluOpType
ACT = mybir.ActivationFunctionType
AX_X = mybir.AxisListType.X

E, N, D = 106250, 6250, 128
P = 128
TILES = 8
GE = P * TILES
G = -(-E // GE)
FULL = E // GE
REST = E - FULL * GE
REST_P, REST_J = REST // TILES, REST % TILES
SLOTS = 4
TURNS = G // SLOTS
EARLY = 2
PEELED = 3
W = 128
PAIRS = TURNS
NB = 2 * PAIRS
BN = -(-N // NB)
PN = 2 * BN
NPAD = NB * BN
LAST_BN = N - (NB - 1) * BN
BASE_MAX = NPAD - W
EPS = 1e-5
ROOT_BITS, NEWTON = 0x5F3759DF, 3
NO_NODE = 30000
DMA = 16
LN0_STEPS, LN1_STEPS = 20, 33
WINDOWS = -(-NPAD // W)


def back(i, u, d):
    return i + (u - d) // SLOTS, (u - d) % SLOTS


def ahead(i, u):
    return i + (u + 1) // SLOTS, (u + 1) % SLOTS


def there(i):
    return not isinstance(i, int) or i >= 0


def is_last(i, u):
    return isinstance(i, int) and SLOTS * i + u == G - 1


def build(nc, x, src, dst, edge, w_msg, b_msg, w_app, b_app, w1, b1, w2, b2, gamma, beta, out):
    ctx = ExitStack()

    def sb(name, shape, dt=F32):
        return ctx.enter_context(nc.sbuf_tensor(name, shape, dt))

    def sem(name):
        return ctx.enter_context(nc.semaphore(name))

    def sems(name, n):
        return [sem(f"{name}{k}") for k in range(n)]

    with ctx:
        table = nc.dram_tensor("table", (NPAD, 2 * D), F32, kind="Internal").ap()
        q_parts = nc.dram_tensor("q_parts", (NPAD, 3 * D), BF16, kind="Internal").ap()
        rel_rows = nc.dram_tensor("rel_rows", (G, GE), BF16, kind="Internal").ap()

        src_g = src[0:FULL * GE].rearrange("(g p j) -> g p j", p=P, j=TILES)
        dst_g = dst[0:FULL * GE].rearrange("(g p j) -> g p j", p=P, j=TILES)
        edge_g = edge[0:FULL * GE, :].rearrange("(g p j) d -> g p (j d)", p=P, j=TILES)
        src_rest, dst_rest = (a[FULL * GE:FULL * GE + REST_P * TILES].rearrange("(p j) -> p j", j=TILES)
                              for a in (src, dst))
        edge_rest = edge[FULL * GE:FULL * GE + REST_P * TILES, :].rearrange("(p j) d -> p (j d)", j=TILES)
        src_end, dst_end = (a[E - REST_J:E].rearrange("(p j) -> p j", p=1) for a in (src, dst))
        edge_end = edge[E - REST_J:E, :].rearrange("(p j) d -> p (j d)", p=1)

        ident = sb("ident", [P, P])
        identb = sb("identb", [P, P], BF16)
        ones = sb("ones", [P, P])
        iota_w = sb("iota_w", [P, W])
        iota_i = sb("iota_i", [P, W], I32)
        iota_pi = sb("iota_pi", [P, 1], I32)
        iota_p = sb("iota_p", [P, 1])
        wmsg_sb = sb("wmsg_sb", [D, 2 * D])
        wapp_sb = sb("wapp_sb", [D, 2 * D])
        wT = sb("wT", [D, 4, D])
        w1_sb = sb("w1_sb", [D, 2 * D])
        rows = sb("rows", [1, 6 * D])
        b2_row = sb("b2_row", [1, 1])
        bcast = sb("bcast", [P, 4, D])
        b2_col = sb("b2_col", [P, 1])
        dst_nat = sb("dst_nat", [G, GE], I32)
        dst_f = sb("dst_f", [G, GE])
        rel_nat = sb("rel_nat", [G, GE], BF16)
        low = sb("low", [G, 1])
        high = sb("high", [G, 1])
        base = sb("base", [G, 1])
        floor_i = sb("floor_i", [G, 1], I32)
        floor = sb("floor", [G, 1])
        spread = sb("spread", [G, 1])
        fits = sb("fits", [G, 2])
        ok = sb("ok", [G, 1])
        base_l = sb("base_l", [G, P])
        base_bc = sb("base_bc", [P, G])
        base_i = sb("base_i", [1, G], I32)
        ok_i = sb("ok_i", [1, 1], I32)
        no_node = sb("no_node", [P, TILES], I32)

        src_slot = sb("src_slot", [P, SLOTS, TILES], I32)
        dst_slot = sb("dst_slot", [P, SLOTS, TILES], I32)
        rel = sb("rel", [P, G * TILES])
        ring = sb("ring", [P, SLOTS, 2 * GE])
        S = sb("S", [P, SLOTS, TILES, W])
        S_sum = sb("S_sum", [P, SLOTS, W])
        acc_x = sb("acc_x", [D, WINDOWS * W])
        acc_e = sb("acc_e", [D, WINDOWS * W])
        acc_deg = sb("acc_deg", [1, WINDOWS * W])
        x_blk = sb("x_blk", [BN, 2, D])
        x_beta = sb("x_beta", [BN, 2, D])
        n_x = sb("n_x", [D, PN])
        n_e = sb("n_e", [D, PN])
        n_deg = sb("n_deg", [1, PN])
        turned = sb("turned", [D, 2 * PN])
        x1T = sb("x1T", [D, PN])
        deg_max = sb("deg_max", [BN, 2])
        deg_inv = sb("deg_inv", [BN, 2])
        z = sb("z", [BN, 2, D])
        y = sb("y", [BN, 2, D])
        stats = sb("stats", [BN, 2, 6])
        moments = sb("moments", [BN, 2, 2])
        var, half, root, newton = (sb(n, [BN, 2]) for n in ("var", "half", "root", "newton"))
        bits = sb("bits", [BN, 2], I32)
        tab_blk = sb("tab_blk", [BN, 2, 2 * D])
        q_blk = sb("q_blk", [BN, 2, 3 * D], BF16)
        q_rest = sb("q_rest", [BN, 2, D])
        rel_bc = sb("rel_bc", [P, SLOTS, GE], BF16)
        ST = sb("ST", [P, SLOTS, TILES, P], BF16)
        q_win = sb("q_win", [P, SLOTS, 3 * D], BF16)
        act_out = sb("act_out", [P, TILES, D])
        logit = sb("logit", [P, SLOTS, TILES])
        weight = sb("weight", [P, SLOTS, TILES])
        fin = sb("fin", [BN, 2, D])
        q_rows = ST[:, :, :, :].rearrange("p s t c -> p (s t c)")[:, 0:3 * GE]

        def bank(name):
            return ctx.enter_context(nc.psum_tensor(name, [P, 512], F32))

        ps_agg = [bank("ps_agg0"), bank("ps_agg1")]
        ps4 = [bank(f"ps4_{k}") for k in range(4)]
        ps_side = bank("ps_side")

        ld_dst, ld_par, memset_ok, iota_ok, acc_zero = (sem(n) for n in ("ld_dst", "ld_par", "memset_ok", "iota_ok", "acc_zero"))
        ident_ok, dve_pro, pe_pro, act_pro = sem("ident_ok"), sem("dve_pro"), sem("pe_pro"), sem("act_pro")
        rel_out = sem("rel_out")
        src_in0, dst_in, edge_in, gath0 = sems("src_in0_", 4), sems("dst_in", 4), sems("edge_in", 4), sems("gath0_", 4)
        pad_in = sem("pad_in")
        rel_done, s_ready, sum_ready, agg0, acc0 = (sem(n) for n in ("rel_done", "s_ready", "sum_ready", "agg0", "acc0"))
        x_in = sem("x_in")
        x_tr, x_cp, cut, prod, prod_cp, mix = (sem(n) for n in ("x_tr", "x_cp", "cut", "prod", "prod_cp", "mix"))
        x1_tr, x1_cp, pq, p_cp, parts = (sem(n) for n in ("x1_tr", "x1_cp", "pq", "p_cp", "parts"))
        q_split, ln0, ln1, tab_out = (sem(n) for n in ("q_split", "ln0", "ln1", "tab_out"))
        cleared = sem("cleared")
        src_in1, gath1, row_in, q_in = sems("src_in1_", 4), sems("gath1_", 4), sems("row_in", 4), sems("q_in", 4)
        st_ready, h_done, dot_done, sig_done, sw_ready, agg1, acc1 = (
            sem(n) for n in ("st_ready", "h_done", "dot_done", "sig_done", "sw_ready", "agg1", "acc1"))
        x1_in, cut1, sum_tr, fin_out, passed = (sem(n) for n in ("x1_in", "cut1", "sum_tr", "fin_out", "passed"))

        def gather_x(u):
            for j in range(TILES):
                nc.gpsimd.indirect_dma_start(
                    out=ring[:, u, j * D:(j + 1) * D], out_offset=None, in_=x,
                    in_offset=bass.IndirectOffsetOnAxis(ap=src_slot[:, u, j:j + 1], axis=0),
                ).then_inc(gath0[u], DMA)

        pro = nc.Block()
        with pro as block:
            @block.sync
            def _(sp):
                for u in range(SLOTS):
                    sp.dma_start(src_slot[:, u, :], src_g[u]).then_inc(src_in0[u], DMA)
                sp.wait_ge(memset_ok, 1)
                sp.dma_start(dst_nat[0:FULL, :], dst[0:FULL * GE].rearrange("(g e) -> g e", e=GE)).then_inc(ld_dst, DMA)
                sp.dma_start(dst_nat[FULL:G, 0:REST], dst[FULL * GE:E].rearrange("(g e) -> g e", g=1)).then_inc(ld_dst, DMA)
                sp.dma_start(wmsg_sb[:, :], w_msg).then_inc(ld_par, DMA)
                sp.dma_start(wapp_sb[:, :], w_app).then_inc(ld_par, DMA)
                for k in range(2):
                    sp.dma_start(w1_sb[:, k * D:(k + 1) * D], w1[k * D:(k + 1) * D, :]).then_inc(ld_par, DMA)
                for k, v in enumerate((b_msg, b_app, b1, w2.rearrange("f o -> (f o)"), gamma, beta)):
                    sp.dma_start(rows[0:1, k * D:(k + 1) * D], v.rearrange("(o f) -> o f", o=1)).then_inc(ld_par, DMA)
                sp.dma_start(b2_row[:, :], b2.rearrange("(o f) -> o f", o=1)).then_inc(ld_par, DMA)
                for u in range(SLOTS):
                    sp.dma_start(dst_slot[:, u, :], dst_g[u]).then_inc(dst_in[u], DMA)
                    sp.dma_start(ring[:, u, GE:2 * GE], edge_g[u]).then_inc(edge_in[u], DMA)
                sp.wait_ge(dve_pro, 4)
                sp.dma_start(rel_rows, rel_nat[:, :]).then_inc(rel_out, DMA)
                sp.wait_ge(rel_out, DMA)

            @block.gpsimd
            def _(pool):
                nc.gpsimd.iota(iota_i[:, :], pattern=[[1, W]], base=0, channel_multiplier=0).then_inc(iota_ok, 1)
                nc.gpsimd.iota(iota_pi[:, :], pattern=[[0, 1]], base=0, channel_multiplier=1).then_inc(iota_ok, 1)
                nc.gpsimd.memset(ident[:, :], 0.0).then_inc(iota_ok, 1)
                pool.wait_ge(iota_ok, 3)
                nc.gpsimd.affine_select(out=ident[:, :], in_=ident[:, :], compare_op=ALU.not_equal, fill=1.0, base=0,
                                        pattern=[[-1, P]], channel_multiplier=1).then_inc(ident_ok, 1)
                for u in range(EARLY):
                    pool.wait_ge(src_in0[u], DMA)
                    gather_x(u)

            @block.vector
            def _(dve):
                nc.vector.memset(dst_nat[:, :], N - 1).then_inc(memset_ok, 1)
                nc.vector.memset(ones[:, :], 1.0).then_inc(memset_ok, 1)
                nc.vector.memset(no_node[:, :], NO_NODE)
                nc.vector.memset(acc_x[:, :], 0.0).then_inc(acc_zero, 1)
                dve.wait_ge(iota_ok, 2)
                nc.vector.tensor_copy(iota_w[:, :], iota_i[:, :])
                nc.vector.tensor_copy(iota_p[:, :], iota_pi[:, :])
                nc.vector.tensor_scalar(floor_i[:, :], iota_pi[0:G, :], 1, None, ALU.arith_shift_right).then_inc(memset_ok, 1)
                dve.wait_ge(memset_ok, 3)
                nc.vector.tensor_scalar(floor[:, :], floor_i[:, :], float(BN), float(-BN), ALU.mult, ALU.add)
                dve.wait_ge(ld_dst, 2 * DMA)
                nc.vector.tensor_copy(dst_f[:, :], dst_nat[:, :]).then_inc(dve_pro, 1)
                dve.wait_ge(dve_pro, 1)
                nc.vector.tensor_reduce(low[:, :], dst_f[:, :], AX_X, ALU.min)
                nc.vector.tensor_reduce(high[:, :], dst_f[:, :], AX_X, ALU.max).then_inc(dve_pro, 1)
                dve.wait_ge(dve_pro, 2)
                nc.vector.tensor_scalar(base[:, :], low[:, :], float(BASE_MAX), None, ALU.min).then_inc(dve_pro, 1)
                dve.wait_ge(dve_pro, 3)
                nc.vector.tensor_scalar(rel_nat[:, :], dst_f[:, :], base[:, 0:1], None, ALU.subtract).then_inc(dve_pro, 1)
                nc.vector.tensor_scalar(base_l[:, :], ones[0:G, :], base[:, 0:1], None, ALU.mult)
                nc.vector.tensor_tensor(spread[:, :], high[:, :], base[:, :], ALU.subtract)
                nc.vector.tensor_tensor(fits[:, 1:2], low[:, :], floor[:, :], ALU.is_ge).then_inc(dve_pro, 1)
                dve.wait_ge(dve_pro, 5)
                nc.vector.tensor_scalar(fits[:, 0:1], spread[:, :], float(W - 1), None, ALU.is_le).then_inc(dve_pro, 1)
                dve.wait_ge(dve_pro, 6)
                nc.vector.tensor_tensor(ok[:, :], fits[:, 0:1], fits[:, 1:2], ALU.mult).then_inc(dve_pro, 1)
                dve.wait_ge(ident_ok, 1)
                nc.vector.tensor_copy(identb[:, :], ident[:, :])
                dve.wait_ge(pe_pro, 2)
                nc.vector.tensor_copy(base_bc[:, :], ps_agg[0][:, 0:G])
                nc.vector.tensor_copy(base_i[:, :], ps_agg[0][0:1, 0:G])
                nc.vector.tensor_copy(ok_i[:, :], ps_agg[1][0:1, 0:1])

            @block.tensor
            def _(pe):
                pe.wait_ge(ident_ok, 1)
                pe.wait_ge(memset_ok, 2)
                pe.wait_ge(ld_par, 11 * DMA)
                for k, w in enumerate((wmsg_sb, wmsg_sb, wapp_sb, wapp_sb)):
                    nc.tensor.transpose(ps4[0][:, k * D:(k + 1) * D], w[:, (k % 2) * D:(k % 2 + 1) * D], ident[:, :])
                nc.tensor.matmul(ps4[1][:, 0:3 * D], ones[0:1, :], rows[0:1, 3 * D:6 * D], start=True, stop=True)
                nc.tensor.matmul(ps4[2][:, 0:1], ones[0:1, :], b2_row[:, :], start=True, stop=True).then_inc(pe_pro, 1)
                pe.wait_ge(dve_pro, 7)
                nc.tensor.matmul(ps_agg[0][:, 0:G], base_l[:, :], ident[0:G, 0:G], start=True, stop=True)
                nc.tensor.matmul(ps_agg[1][0:1, 0:1], ok[:, :], ones[0:G, 0:1], start=True, stop=True).then_inc(pe_pro, 1)

            @block.scalar
            def _(act):
                act.wait_ge(acc_zero, 1)
                nc.scalar.copy(acc_e[:, :], acc_x[:, :])
                nc.scalar.copy(acc_deg[:, :], acc_x[0:1, :])
                act.wait_ge(pe_pro, 1)
                nc.scalar.copy(wT[:, :, :].rearrange("p a b -> p (a b)"), ps4[0][:, :])
                nc.scalar.copy(bcast[:, 0:3, :].rearrange("p a b -> p (a b)"), ps4[1][:, 0:3 * D])
                nc.scalar.copy(bcast[:, 3, :], ps4[1][:, 2 * D:3 * D])
                nc.scalar.copy(b2_col[:, :], ps4[2][:, 0:1])

        fitting = nc.values_load(ok_i[0:1, 0:1], min_val=0, max_val=G)

        waT, wbT, wcT, wdT = (wT[:, k, :] for k in range(4))
        b_msg_row, b_app_row, b1_row = (rows[0:1, k * D:(k + 1) * D] for k in range(3))
        w2_bc, gamma_bc, beta_bc = bcast[:, 0, :], bcast[0:BN, 1, :], bcast[0:BN, 2:4, :]

        def wait_apart(eng, semaphore, value):
            eng.wait_ge(semaphore, value)
            eng.sem_inc(passed, 1)

        def dve_moments(dve, done, at, values):
            for v in range(2):
                last = nc.vector.bn_stats(stats[:, v, :], values[:, v, :])
            last.then_inc(done, 1)
            wait_apart(dve, done, at + 1)
            for v in range(2):
                last = nc.vector.bn_aggr(moments[:, v, :], stats[:, v, :])
            last.then_inc(done, 1)

        def dve_root(dve, done, at):
            dve.wait_ge(done, at)
            nc.vector.tensor_scalar(var[:, :], moments[:, :, 1], EPS, None, ALU.add).then_inc(done, 1)
            dve.wait_ge(done, at + 1)
            nc.vector.tensor_scalar(half[:, :], var[:, :], -0.5, None, ALU.mult)
            nc.vector.tensor_scalar(bits[:, :], var[:, :].bitcast(I32), 1, None, ALU.arith_shift_right).then_inc(done, 1)
            dve.wait_ge(done, at + 2)
            nc.vector.tensor_scalar(root[:, :].bitcast(I32), bits[:, :], -1.0, float(ROOT_BITS), ALU.mult, ALU.add).then_inc(done, 1)
            for k in range(NEWTON):
                dve.wait_ge(done, at + 3 * k + 3)
                nc.vector.tensor_tensor(newton[:, :], root[:, :], half[:, :], ALU.mult).then_inc(done, 1)
                dve.wait_ge(done, at + 3 * k + 4)
                nc.vector.tensor_tensor(newton[:, :], newton[:, :], root[:, :], ALU.mult).then_inc(done, 1)
                dve.wait_ge(done, at + 3 * k + 5)
                nc.vector.scalar_tensor_tensor(root[:, :], newton[:, :], 1.5, root[:, :], ALU.add, ALU.mult).then_inc(done, 1)

        def dve_normalise(dve, done, at, values, result):
            dve.wait_ge(done, at)
            for v in range(2):
                last = nc.vector.tensor_scalar(result[:, v, :], values[:, v, :], moments[:, v, 0:1], root[:, v:v + 1],
                                               ALU.subtract, ALU.mult)
            last.then_inc(done, 1)

        def pair_rows(dram, t):
            return dram[bass.ds(PN * t, PN), :].rearrange("(v p) c -> p v c", p=BN)

        def sp_x_pair(sp, t, last=False):
            if there(t - 1):
                wait_apart(sp, ln0, LN0_STEPS * (t - 1) + 5)
                sp.wait_ge(x_tr, t)
            if last:
                sp.dma_start(x_blk[:, 0, :], x[PN * t:PN * t + BN, :]).then_inc(x_in, DMA)
                sp.dma_start(x_blk[0:LAST_BN, 1, :], x[PN * t + BN:N, :]).then_inc(x_in, DMA)
            else:
                sp.dma_start(x_blk[:, :, :], pair_rows(x, t)).then_inc(x_in, DMA)

        def act_cut0(act, t):
            if there(t - 1):
                act.wait_ge(mix, t)
            for to, of, n in ((n_x, acc_x, D), (n_e, acc_e, D), (n_deg, acc_deg, 1)):
                last = nc.scalar.copy(to[0:n, :], of[0:n, bass.ds(PN * t, PN)])
            last.then_inc(cut, 1)

        def pe_x0(pe, t, final=False):
            pe.wait_ge(x_in, DMA * (t + 1 + final))
            for v in range(2):
                last = nc.tensor.transpose(ps_side[:, BN * v:BN * (v + 1)], x_blk[:, v, :], ident[0:BN, 0:BN])
            last.then_inc(x_tr, 1)
            pe.wait_ge(x_cp, t + 1)
            for v in range(2):
                app = ps4[2][0:BN, (2 + v) * D:(3 + v) * D]
                nc.tensor.matmul(app, turned[:, PN + BN * v:PN + BN * (v + 1)], wcT, start=True, stop=False)
                nc.tensor.matmul(app, ones[0:1, 0:BN], b_app_row, start=False, stop=True)

        def act_x0(act, t):
            act.wait_ge(x_tr, t + 1)
            if there(t - 1):
                act.wait_ge(mix, t)
            nc.scalar.copy(turned[:, PN:2 * PN], ps_side[:, 0:PN]).then_inc(x_cp, 1)

        def pe_products0(pe, t):
            pe.wait_ge(cut, t + 1)
            if there(t - 1):
                pe.wait_ge(parts, t)
            hs = ps4[0][:, 0:PN]
            nc.tensor.matmul(hs, waT, n_x[:, :], start=True, stop=False)
            nc.tensor.matmul(hs, wbT, n_e[:, :], start=False, stop=False)
            nc.tensor.matmul(hs, b_msg_row, n_deg[:, :], start=False, stop=True).then_inc(prod, 1)

        def act_products0(act, t):
            act.wait_ge(prod, t + 1)
            nc.scalar.copy(turned[:, 0:PN], ps4[0][:, 0:PN]).then_inc(prod_cp, 1)

        def pe_mix0(pe, t):
            for v in range(2):
                nc.tensor.matmul(ps4[1][0:BN, v:v + 1], n_deg[:, BN * v:BN * (v + 1)], ones[0:1, 0:1], start=True, stop=True)
            pe.wait_ge(prod_cp, t + 1)
            for v in range(2):
                last = nc.tensor.matmul(ps4[2][0:BN, v * D:(v + 1) * D], turned[:, BN * v:BN * (v + 1)], wdT,
                                        start=True, stop=True)
            last.then_inc(mix, 1)

        def dve_sum0(dve, t):
            at = LN0_STEPS * t
            dve.wait_ge(mix, t + 1)
            nc.vector.tensor_scalar(deg_max[:, :], ps4[1][0:BN, 0:2], 1.0, None, ALU.max).then_inc(ln0, 1)
            dve.wait_ge(ln0, at + 1)
            nc.vector.reciprocal(deg_inv[:, :], deg_max[:, :]).then_inc(ln0, 1)
            dve.wait_ge(ln0, at + 2)
            hs, app = (ps4[2][0:BN, 2 * D * k:2 * D * (k + 1)].rearrange("p (v d) -> p v d", v=2) for k in range(2))
            for v in range(2):
                last = nc.vector.tensor_scalar(z[:, v, :], hs[:, v, :], deg_inv[:, v:v + 1], None, ALU.mult)
            last.then_inc(ln0, 1)
            dve.wait_ge(ln0, at + 3)
            nc.vector.tensor_tensor(z[:, :, :], z[:, :, :], app, ALU.add).then_inc(ln0, 1)
            dve.wait_ge(ln0, at + 4)
            nc.vector.scalar_tensor_tensor(y[:, :, :], z[:, :, :], 0.0, x_blk[:, :, :], ALU.max, ALU.add).then_inc(ln0, 1)
            dve.wait_ge(ln0, at + 5)
            dve_moments(dve, ln0, at + 5, y)

        def dve_norm0(dve, t):
            at = LN0_STEPS * t
            if there(t - 1):
                dve.wait_ge(tab_out, 2 * DMA * t)
            dve_root(dve, ln0, at + 7)
            dve_normalise(dve, ln0, at + 19, y, tab_blk[:, :, 0:D])

        def pe_turn0(pe, t):
            pe.wait_ge(ln0, LN0_STEPS * (t + 1))
            for v in range(2):
                last = nc.tensor.transpose(ps4[1][:, BN * v:BN * (v + 1)], tab_blk[:, v, 0:D], ident[0:BN, 0:BN])
            last.then_inc(x1_tr, 1)

        def act_turn0(act, t):
            act.wait_ge(x1_tr, t + 1)
            if there(t - 1):
                act.wait_ge(pq, t)
            nc.scalar.copy(x1T[:, :], ps4[1][:, 0:PN]).then_inc(x1_cp, 1)

        def pe_pq0(pe, t):
            pe.wait_ge(x1_cp, t + 1)
            if there(t - 1):
                pe.wait_ge(p_cp, t)
            for v in range(2):
                x1_v, cols = x1T[:, BN * v:BN * (v + 1)], slice(v * D, (v + 1) * D)
                nc.tensor.matmul(ps4[0][0:BN, cols], x1_v, w1_sb[:, D:2 * D], start=True, stop=True)
                nc.tensor.matmul(ps4[3][0:BN, cols], x1_v, w1_sb[:, 0:D], start=True, stop=False)
                last = nc.tensor.matmul(ps4[3][0:BN, cols], ones[0:1, 0:BN], b1_row, start=False, stop=True)
            last.then_inc(pq, 1)

        def dve_parts0(dve, t):
            q = ps4[0][0:BN, 0:2 * D].rearrange("p (v d) -> p v d", v=2)
            hi, mid, lo = (q_blk[:, :, k * D:(k + 1) * D] for k in range(3))
            dve.wait_ge(pq, t + 1)
            if there(t - 1):
                dve.wait_ge(tab_out, 2 * DMA * t)
            nc.vector.tensor_copy(hi, q).then_inc(q_split, 1)
            dve.wait_ge(q_split, 3 * t + 1)
            nc.vector.tensor_tensor(q_rest[:, :, :], q, hi, ALU.subtract).then_inc(q_split, 1)
            dve.wait_ge(q_split, 3 * t + 2)
            nc.vector.tensor_copy(mid, q_rest[:, :, :]).then_inc(q_split, 1)
            dve.wait_ge(q_split, 3 * t + 3)
            nc.vector.tensor_tensor(lo, q_rest[:, :, :], mid, ALU.subtract).then_inc(parts, 1)

        def act_store0(act, t):
            act.wait_ge(pq, t + 1)
            if there(t - 1):
                act.wait_ge(tab_out, 2 * DMA * t)
            nc.scalar.copy(tab_blk[:, :, D:2 * D], ps4[3][0:BN, 0:2 * D].rearrange("p (v d) -> p v d", v=2)).then_inc(p_cp, 1)
            act.wait_ge(p_cp, t + 1)
            act.dma_start(pair_rows(table, t), tab_blk[:, :, :]).then_inc(tab_out, DMA)
            act.wait_ge(parts, t + 1)
            act.dma_start(pair_rows(q_parts, t), q_blk[:, :, :]).then_inc(tab_out, DMA)

        def sp_x1_pair(sp, t):
            if there(t - 1):
                sp.wait_ge(ln1, LN1_STEPS * (t - 1) + 2)
            sp.dma_start(x_blk[:, :, :], pair_rows(table, t)[:, :, 0:D]).then_inc(x1_in, DMA)

        def act_cut1(act, t):
            if there(t - 1):
                act.wait_ge(sum_tr, t)
            nc.scalar.copy(n_x[:, :], acc_x[:, bass.ds(PN * t, PN)]).then_inc(cut1, 1)

        def pe_turn1(pe, t):
            pe.wait_ge(cut1, t + 1)
            if there(t - 1):
                pe.wait_ge(ln1, LN1_STEPS * (t - 1) + 1)
            for v in range(2):
                last = nc.tensor.transpose(ps_side[0:BN, D * v:D * (v + 1)], n_x[:, BN * v:BN * (v + 1)], ident[:, :])
            last.then_inc(sum_tr, 1)

        def dve_first1(dve, t):
            at = LN1_STEPS * t
            dve.wait_ge(sum_tr, t + 1)
            dve.wait_ge(x1_in, DMA * (t + 1))
            nc.vector.tensor_tensor(z[:, :, :], ps_side[0:BN, 0:2 * D].rearrange("p (v d) -> p v d", v=2), x_blk[:, :, :],
                                    ALU.add).then_inc(ln1, 1)
            nc.vector.tensor_tensor(x_beta[:, :, :], x_blk[:, :, :], beta_bc, ALU.add).then_inc(ln1, 1)
            dve.wait_ge(ln1, at + 2)
            dve_moments(dve, ln1, at + 2, z)
            dve.wait_ge(ln1, at + 4)
            for v in range(2):
                last = nc.vector.scalar_tensor_tensor(y[:, v, :], z[:, v, :], moments[:, v, 0:1], gamma_bc, ALU.subtract, ALU.mult)
            last.then_inc(ln1, 1)

        def dve_second1(dve, t):
            at = LN1_STEPS * t
            dve_root(dve, ln1, at + 5)
            dve.wait_ge(ln1, at + 17)
            for v in range(2):
                last = nc.vector.scalar_tensor_tensor(z[:, v, :], y[:, v, :], root[:, v:v + 1], x_beta[:, v, :], ALU.mult, ALU.add)
            last.then_inc(ln1, 1)
            dve.wait_ge(ln1, at + 18)
            dve_moments(dve, ln1, at + 18, z)

        def dve_third1(dve, t):
            at = LN1_STEPS * t
            if there(t - 1):
                dve.wait_ge(fin_out, DMA * t)
            dve_root(dve, ln1, at + 20)
            dve_normalise(dve, ln1, at + 32, z, fin)

        def act_store1(act, t, last=False):
            act.wait_ge(ln1, LN1_STEPS * (t + 1))
            if last:
                act.dma_start(out[PN * t:PN * t + BN, :], fin[:, 0, :]).then_inc(fin_out, DMA)
                act.dma_start(out[PN * t + BN:N, :], fin[0:LAST_BN, 1, :]).then_inc(fin_out, DMA)
            else:
                act.dma_start(pair_rows(out, t), fin[:, :, :]).then_inc(fin_out, DMA)

        def accumulate(dve, psum_cols, into, at):
            return nc.vector.tensor_tensor(into[:, bass.ds(at, W)], into[:, bass.ds(at, W)], psum_cols, ALU.add)

        def tables_stored(eng):
            eng.wait_ge(tab_out, PAIRS * 2 * DMA)

        def dve_logits(dve, u, g, first_bank):
            for j in range(TILES):
                if j % 4 == 0:
                    dve.wait_ge(h_done, 2 * g + 1 + j // 4)
                cols = ps4[first_bank + j // 4][:, (j % 4) * D:(j % 4 + 1) * D]
                last = nc.vector.scalar_tensor_tensor(act_out[:, j, :], cols, 0.0, w2_bc, ALU.max, ALU.mult,
                                                      accum_out=logit[:, u, j:j + 1])
            last.then_inc(dot_done, 1)

        def act_weights(act, u, g):
            act.wait_ge(dot_done, g + 1)
            nc.scalar.activation(weight[:, u, :], logit[:, u, :], ACT.Sigmoid, bias=b2_col[:, 0:1]).then_inc(sig_done, 1)

        def windowed():
            def sp_layer0(sp):
                def load(i, u, last=False):
                    g = SLOTS * i + u
                    sp.wait_ge(gath0[u], TILES * DMA * i)
                    if last:
                        sp.dma_start(src_slot[0:REST_P, u, :], src_rest).then_inc(src_in0[u], DMA)
                        sp.dma_start(src_slot[REST_P:REST_P + 1, u, 0:REST_J], src_end).then_inc(src_in0[u], DMA)
                    else:
                        sp.dma_start(src_slot[:, u, :], src_g[g]).then_inc(src_in0[u], DMA)
                    sp.wait_ge(rel_done, g - SLOTS + 1)
                    if last:
                        sp.dma_start(dst_slot[:, u, :], no_node[:, :]).then_inc(pad_in, DMA)
                        sp.wait_ge(pad_in, DMA)
                        sp.dma_start(dst_slot[0:REST_P, u, :], dst_rest).then_inc(dst_in[u], DMA)
                        sp.dma_start(dst_slot[REST_P:REST_P + 1, u, 0:REST_J], dst_end).then_inc(dst_in[u], DMA)
                    else:
                        sp.dma_start(dst_slot[:, u, :], dst_g[g]).then_inc(dst_in[u], DMA)
                    sp.wait_ge(agg0, g - SLOTS + 1)
                    if last:
                        sp.dma_start(ring[0:REST_P, u, GE:2 * GE], edge_rest).then_inc(edge_in[u], DMA)
                        sp.dma_start(ring[REST_P:REST_P + 1, u, GE:GE + REST_J * D], edge_end).then_inc(edge_in[u], DMA)
                    else:
                        sp.dma_start(ring[:, u, GE:2 * GE], edge_g[g]).then_inc(edge_in[u], DMA)
                    if u == SLOTS - 1:
                        sp_x_pair(sp, i - 1)

                for n in range(SLOTS, PEELED * SLOTS):
                    load(*divmod(n, SLOTS))
                with sp.Fori(PEELED, TURNS - 1) as i:
                    for u in range(SLOTS):
                        load(i, u)
                for u in range(SLOTS):
                    load(TURNS - 1, u, last=u == SLOTS - 1)
                sp_x_pair(sp, PAIRS - 1, last=True)

            def pool_layer0(pool):
                def gather(i, u):
                    g = SLOTS * i + u
                    pool.wait_ge(src_in0[u], DMA * (i + 1 + is_last(i, u)))
                    if there(i - 1):
                        wait_apart(pool, agg0, g - SLOTS + 1)
                    gather_x(u)

                for n in range(EARLY, PEELED * SLOTS):
                    gather(*divmod(n, SLOTS))
                with pool.Fori(PEELED, TURNS - 1) as i:
                    for u in range(SLOTS):
                        gather(i, u)
                for u in range(SLOTS):
                    gather(TURNS - 1, u)

            def dve_layer0(dve):
                def sums(i, u):
                    g = SLOTS * i + u
                    at = dve.value_load(base_i[0:1, bass.ds(g, 1)], min_val=0, max_val=BASE_MAX)
                    dve.wait_ge(agg0, g + 1)
                    if there(g - 1):
                        dve.wait_ge(acc0, g)
                    ps = ps_agg[u % 2]
                    accumulate(dve, ps[:, 0:W], acc_x, at)
                    accumulate(dve, ps[:, W:2 * W], acc_e, at)
                    accumulate(dve, ps[0:1, 2 * W:3 * W], acc_deg, at).then_inc(acc0, 1)

                def one_hots(i, u):
                    g = SLOTS * i + u
                    dve.wait_ge(dst_in[u], DMA * (i + 1 + is_last(i, u)))
                    nc.vector.tensor_scalar(rel[:, bass.ds(TILES * g, TILES)], dst_slot[:, u, :],
                                            base_bc[:, bass.ds(g, 1)], None, ALU.subtract).then_inc(rel_done, 1)
                    dve.wait_ge(rel_done, g + 1)
                    if there(i - 1):
                        dve.wait_ge(agg0, g - SLOTS + 1)
                    for j in range(TILES):
                        last = nc.vector.tensor_scalar(S[:, u, j, :], iota_w[:, :],
                                                       rel[:, bass.ds(TILES * g + j, 1)], None, ALU.is_equal)
                    last.then_inc(s_ready, 1)
                    dve.wait_ge(s_ready, g + 1)
                    nc.vector.tensor_reduce(S_sum[:, u, :], S[:, u, :, :].rearrange("p j w -> p w j"), AX_X,
                                            ALU.add).then_inc(sum_ready, 1)

                def step(i, u):
                    if not is_last(i, u):
                        one_hots(*ahead(i, u))
                    if u == 3 and there(i - 1):
                        dve_sum0(dve, i - 1)
                        dve_norm0(dve, i - 1)
                    if u == 0 and there(i - 2):
                        dve_parts0(dve, i - 2)
                    before = back(i, u, 1)
                    if there(before[0]):
                        sums(*before)

                one_hots(0, 0)
                for n in range(PEELED * SLOTS):
                    step(*divmod(n, SLOTS))
                with dve.Fori(PEELED, TURNS - 1) as i:
                    for u in range(SLOTS):
                        step(i, u)
                for u in range(SLOTS):
                    step(TURNS - 1, u)
                sums(TURNS - 1, SLOTS - 1)
                dve_parts0(dve, PAIRS - 2)
                for phase in (dve_sum0, dve_norm0, dve_parts0):
                    phase(dve, PAIRS - 1)

            def pe_layer0(pe):
                def summed(u, at, lhs_at):
                    for j in range(TILES):
                        last = nc.tensor.matmul(ps_agg[u % 2][:, at:at + W],
                                                ring[:, u, lhs_at + j * D:lhs_at + (j + 1) * D], S[:, u, j, :],
                                                start=j == 0, stop=j == TILES - 1)
                    return last

                def step(i, u):
                    g = SLOTS * i + u
                    if u == 0 and there(i - 2):
                        pe_pq0(pe, i - 2)
                    if u == 2 and there(i - 1):
                        pe_x0(pe, i - 1)
                        pe_products0(pe, i - 1)
                    pe.wait_ge(edge_in[u], DMA * (i + 1 + is_last(i, u)))
                    pe.wait_ge(s_ready, g + 1)
                    if there(g - 2):
                        pe.wait_ge(acc0, g - 1)
                    summed(u, W, GE)
                    pe.wait_ge(sum_ready, g + 1)
                    nc.tensor.matmul(ps_agg[u % 2][0:1, 2 * W:3 * W], ones[:, 0:1], S_sum[:, u, :], start=True, stop=True)
                    if u == 2 and there(i - 1):
                        pe_mix0(pe, i - 1)
                    pe.wait_ge(gath0[u], TILES * DMA * (i + 1))
                    summed(u, 0, 0).then_inc(agg0, 1)
                    if u == 3 and there(i - 1):
                        pe_turn0(pe, i - 1)

                for n in range(PEELED * SLOTS):
                    step(*divmod(n, SLOTS))
                with pe.Fori(PEELED, TURNS - 1) as i:
                    for u in range(SLOTS):
                        step(i, u)
                for u in range(SLOTS):
                    step(TURNS - 1, u)
                pe_pq0(pe, PAIRS - 2)
                pe_x0(pe, PAIRS - 1, final=True)
                for phase in (pe_products0, pe_mix0, pe_turn0, pe_pq0):
                    phase(pe, PAIRS - 1)

            def act_layer0(act):
                def step(i, u):
                    if u == 0 and there(i - 2):
                        act_store0(act, i - 2)
                    if u == 2 and there(i - 1):
                        act_x0(act, i - 1)
                        act.wait_ge(acc0, SLOTS * i + 2)
                        act_cut0(act, i - 1)
                        act_products0(act, i - 1)
                    if u == 3 and there(i - 1):
                        act_turn0(act, i - 1)

                for n in range(PEELED * SLOTS):
                    step(*divmod(n, SLOTS))
                with act.Fori(PEELED, TURNS) as i:
                    for u in range(SLOTS):
                        step(i, u)
                act_x0(act, PAIRS - 1)
                act.wait_ge(acc0, G)
                act_cut0(act, PAIRS - 1)
                act_store0(act, PAIRS - 2)
                for phase in (act_products0, act_turn0, act_store0):
                    phase(act, PAIRS - 1)

            def sp_layer1(sp):
                def load_window(i, u):
                    g = SLOTS * i + u
                    at = sp.value_load(base_i[0:1, bass.ds(g, 1)], min_val=0, max_val=BASE_MAX)
                    if there(i - 1):
                        sp.wait_ge(h_done, 2 * (g - SLOTS + 1))
                    sp.dma_start(q_win[:, u, :], q_parts[bass.ds(at, W), :]).then_inc(q_in[u], DMA)

                def load(i, u, last=False):
                    g = SLOTS * i + u
                    if there(i - 1):
                        sp.wait_ge(gath1[u], TILES * DMA * i)
                    else:
                        sp.wait_ge(gath0[u], TILES * DMA * TURNS)
                    if last:
                        sp.dma_start(src_slot[0:REST_P, u, :], src_rest).then_inc(src_in1[u], DMA)
                        sp.dma_start(src_slot[REST_P:REST_P + 1, u, 0:REST_J], src_end).then_inc(src_in1[u], DMA)
                    else:
                        sp.dma_start(src_slot[:, u, :], src_g[g]).then_inc(src_in1[u], DMA)
                    if there(i - 1):
                        wait_apart(sp, st_ready, g - SLOTS + 1)
                    sp.dma_start(rel_bc[:, u, :], rel_rows[bass.ds(g, 1), :].to_broadcast([P, GE])).then_inc(row_in[u], DMA)
                    if there(i - 1):
                        load_window(i, u)
                    if u == SLOTS - 1 and there(i - 1):
                        sp_x1_pair(sp, i - 1)

                for u in range(SLOTS):
                    load(0, u)
                tables_stored(sp)
                for u in range(SLOTS):
                    load_window(0, u)
                for n in range(SLOTS, PEELED * SLOTS):
                    load(*divmod(n, SLOTS))
                with sp.Fori(PEELED, TURNS - 1) as i:
                    for u in range(SLOTS):
                        load(i, u)
                for u in range(SLOTS):
                    load(TURNS - 1, u, last=u == SLOTS - 1)
                sp_x1_pair(sp, PAIRS - 1)

            def pool_layer1(pool):
                def gather(i, u):
                    g = SLOTS * i + u
                    pool.wait_ge(src_in1[u], DMA * (i + 1 + is_last(i, u)))
                    if there(i - 1):
                        wait_apart(pool, agg1, g - SLOTS + 1)
                    for j in range(TILES):
                        nc.gpsimd.indirect_dma_start(
                            out=ring[:, u, 2 * j * D:2 * (j + 1) * D], out_offset=None, in_=table,
                            in_offset=bass.IndirectOffsetOnAxis(ap=src_slot[:, u, j:j + 1], axis=0),
                        ).then_inc(gath1[u], DMA)

                tables_stored(pool)
                pool.wait_ge(agg0, G)
                for n in range(PEELED * SLOTS):
                    gather(*divmod(n, SLOTS))
                with pool.Fori(PEELED, TURNS - 1) as i:
                    for u in range(SLOTS):
                        gather(i, u)
                for u in range(SLOTS):
                    gather(TURNS - 1, u)

            def dve_layer1(dve):
                def sums(i, u):
                    g = SLOTS * i + u
                    at = dve.value_load(base_i[0:1, bass.ds(g, 1)], min_val=0, max_val=BASE_MAX)
                    dve.wait_ge(agg1, g + 1)
                    if there(g - 1):
                        dve.wait_ge(acc1, g)
                    accumulate(dve, ps_agg[u % 2][:, 0:W], acc_x, at).then_inc(acc1, 1)

                def one_hots(i, u):
                    g = SLOTS * i + u
                    dve.wait_ge(row_in[u], DMA * (i + 1))
                    if there(i - 1):
                        dve.wait_ge(h_done, 2 * (g - SLOTS + 1))
                    nc.vector.tensor_scalar(ST[:, u, :, :].rearrange("w j p -> w p j"),
                                            rel_bc[:, u, :].rearrange("w (p j) -> w p j", j=TILES),
                                            iota_p[:, 0:1], None, ALU.is_equal).then_inc(st_ready, 1)

                def step(i, u):
                    if not is_last(i, u):
                        one_hots(*ahead(i, u))
                    before, two_before = back(i, u, 1), back(i, u, 2)
                    if there(before[0]):
                        dve_logits(dve, before[1], SLOTS * before[0] + before[1], 2 * (before[1] % 2))
                    if there(two_before[0]):
                        sums(*two_before)
                    if there(before[0]):
                        weigh(*before)
                    if u == 3 and there(i - 1):
                        dve_first1(dve, i - 1)
                    if u == 0 and there(i - 2):
                        dve_second1(dve, i - 2)
                    if u == 1 and there(i - 2):
                        dve_third1(dve, i - 2)

                def weigh(i, u):
                    g = SLOTS * i + u
                    dve.wait_ge(sig_done, g + 1)
                    if there(i - 1):
                        dve.wait_ge(agg1, g - SLOTS + 1)
                    for j in range(TILES):
                        last = nc.vector.tensor_scalar(S[:, u, j, :], iota_w[:, :], rel[:, bass.ds(TILES * g + j, 1)],
                                                       weight[:, u, j:j + 1], ALU.is_equal, ALU.mult)
                    last.then_inc(sw_ready, 1)

                one_hots(0, 0)
                dve.wait_ge(cut, PAIRS)
                nc.vector.memset(acc_x[:, :], 0.0).then_inc(cleared, 1)
                dve.wait_ge(cleared, 1)
                for n in range(PEELED * SLOTS):
                    step(*divmod(n, SLOTS))
                with dve.Fori(PEELED, TURNS - 1) as i:
                    for u in range(SLOTS):
                        step(i, u)
                for u in range(SLOTS):
                    step(TURNS - 1, u)
                dve_second1(dve, PAIRS - 2)
                dve_logits(dve, SLOTS - 1, G - 1, 2)
                sums(TURNS - 1, SLOTS - 2)
                weigh(TURNS - 1, SLOTS - 1)
                dve_third1(dve, PAIRS - 2)
                sums(TURNS - 1, SLOTS - 1)
                for phase in (dve_first1, dve_second1, dve_third1):
                    phase(dve, PAIRS - 1)

            def pe_layer1(pe):
                def pre_activation(i, u):
                    g = SLOTS * i + u
                    pe.wait_ge(gath1[u], TILES * DMA * (i + 1))
                    pe.wait_ge(q_in[u], DMA * (i + 1))
                    pe.wait_ge(st_ready, g + 1)
                    if there(g - 2):
                        pe.wait_ge(dot_done, g - 1)
                    for j in range(TILES):
                        cols = ps4[2 * (u % 2) + j // 4][:, (j % 4) * D:(j % 4 + 1) * D]
                        nc.tensor.matmul(cols, ident[:, :], ring[:, u, (2 * j + 1) * D:(2 * j + 2) * D], start=True, stop=False)
                        for k in range(3):
                            last = nc.tensor.matmul(cols, ST[:, u, j, :], q_win[:, u, k * D:(k + 1) * D],
                                                    start=False, stop=k == 2)
                        if j % 4 == 3:
                            last.then_inc(h_done, 1)

                def summed(i, u):
                    g = SLOTS * i + u
                    pe.wait_ge(sw_ready, g + 1)
                    if there(g - 2):
                        pe.wait_ge(acc1, g - 1)
                    for j in range(TILES):
                        last = nc.tensor.matmul(ps_agg[u % 2][:, 0:W], ring[:, u, 2 * j * D:(2 * j + 1) * D],
                                                S[:, u, j, :], start=j == 0, stop=j == TILES - 1)
                    last.then_inc(agg1, 1)

                def step(i, u):
                    if u == 3 and there(i - 1):
                        pe_turn1(pe, i - 1)
                    pre_activation(i, u)
                    before = back(i, u, 1)
                    if there(before[0]):
                        summed(*before)

                pe.wait_ge(parts, PAIRS)
                pe.wait_ge(p_cp, PAIRS)
                pe.wait_ge(acc0, G)
                pe.wait_ge(x_cp, PAIRS)
                for n in range(PEELED * SLOTS):
                    step(*divmod(n, SLOTS))
                with pe.Fori(PEELED, TURNS) as i:
                    for u in range(SLOTS):
                        step(i, u)
                summed(TURNS - 1, SLOTS - 1)
                pe_turn1(pe, PAIRS - 1)

            def act_layer1(act):
                def step(i, u):
                    before = back(i, u, 1)
                    if there(before[0]):
                        act_weights(act, before[1], SLOTS * before[0] + before[1])
                    if u == 3 and there(i - 1):
                        act.wait_ge(acc1, SLOTS * i + 2)
                        act_cut1(act, i - 1)
                    if u == 2 and there(i - 2):
                        act_store1(act, i - 2)

                act.wait_ge(mix, PAIRS)
                for n in range(PEELED * SLOTS):
                    step(*divmod(n, SLOTS))
                with act.Fori(PEELED, TURNS) as i:
                    for u in range(SLOTS):
                        step(i, u)
                act_weights(act, SLOTS - 1, G - 1)
                act_store1(act, PAIRS - 2)
                act.wait_ge(acc1, G)
                act_cut1(act, PAIRS - 1)
                act_store1(act, PAIRS - 1, last=True)
                act.wait_ge(fin_out, DMA * (PAIRS + 1))

            with nc.Block() as block:
                @block.sync
                def _(sp):
                    sp_layer0(sp)
                    sp_layer1(sp)

                @block.gpsimd
                def _(pool):
                    pool_layer0(pool)
                    pool_layer1(pool)

                @block.vector
                def _(dve):
                    dve_layer0(dve)
                    dve_layer1(dve)

                @block.tensor
                def _(pe):
                    pe_layer0(pe)
                    pe_layer1(pe)

                @block.scalar
                def _(act):
                    act_layer0(act)
                    act_layer1(act)

        def general():
            def groups(eng, step, first=0):
                with eng.Fori(first, G - 1) as g:
                    step(g, False)
                step(G - 1, True)

            def pairs(eng, *phases):
                def pair(t):
                    for phase in phases:
                        phase(eng, t)

                pair(0)
                with eng.Fori(1, PAIRS - 1) as t:
                    pair(t)
                pair(PAIRS - 1)

            def is_last_pair(t):
                return isinstance(t, int) and t == PAIRS - 1

            def load_indices(sp, g, last, acc, src_in):
                sp.wait_ge(acc, WINDOWS * g + 1)
                if last:
                    sp.dma_start(src_slot[0:REST_P, 0, :], src_rest).then_inc(src_in, DMA)
                    sp.dma_start(src_slot[REST_P:REST_P + 1, 0, 0:REST_J], src_end).then_inc(src_in, DMA)
                    sp.dma_start(dst_slot[:, 0, :], no_node[:, :]).then_inc(pad_in, DMA)
                    sp.wait_ge(pad_in, DMA if acc is acc0 else 2 * DMA)
                    sp.dma_start(dst_slot[0:REST_P, 0, :], dst_rest).then_inc(dst_in[0], DMA)
                    sp.dma_start(dst_slot[REST_P:REST_P + 1, 0, 0:REST_J], dst_end).then_inc(dst_in[0], DMA)
                else:
                    sp.dma_start(src_slot[:, 0, :], src_g[g]).then_inc(src_in, DMA)
                    sp.dma_start(dst_slot[:, 0, :], dst_g[g]).then_inc(dst_in[0], DMA)

            def start_windows(dve, g, last, groups_before):
                dve.wait_ge(dst_in[0], DMA * (groups_before + g + 1 + last))
                nc.vector.tensor_scalar(rel[:, 0:TILES], dst_slot[:, 0, :], float(W), None, ALU.add).then_inc(rel_done, 1)

            def next_window(dve, n):
                dve.wait_ge(rel_done, n)
                nc.vector.tensor_scalar(rel[:, 0:TILES], rel[:, 0:TILES], float(-W), None, ALU.add).then_inc(rel_done, 1)
                dve.wait_ge(rel_done, n + 1)

            REL_STEPS = WINDOWS + 1
            L1_REL = G * REL_STEPS

            with nc.Block() as block:
                @block.sync
                def _(sp):
                    def step(g, last):
                        load_indices(sp, g, last, acc0, src_in0[0])
                        if last:
                            sp.dma_start(ring[0:REST_P, 0, GE:2 * GE], edge_rest).then_inc(edge_in[0], DMA)
                            sp.dma_start(ring[REST_P:REST_P + 1, 0, GE:GE + REST_J * D], edge_end).then_inc(edge_in[0], DMA)
                        else:
                            sp.dma_start(ring[:, 0, GE:2 * GE], edge_g[g]).then_inc(edge_in[0], DMA)

                    groups(sp, step, first=1)

                @block.gpsimd
                def _(pool):
                    def step(g, last):
                        wait_apart(pool, src_in0[0], DMA * (g + 1 + last))
                        wait_apart(pool, acc0, WINDOWS * g + 1)
                        gather_x(0)

                    groups(pool, step, first=1)

                @block.vector
                def _(dve):
                    def step(g, last):
                        start_windows(dve, g, last, 0)
                        with dve.Fori(0, WINDOWS) as k:
                            n = WINDOWS * g + k
                            next_window(dve, REL_STEPS * g + k + 1)
                            for j in range(TILES):
                                done = nc.vector.tensor_scalar(S[:, 0, j, :], iota_w[:, :], rel[:, j:j + 1], None, ALU.is_equal)
                            done.then_inc(s_ready, 1)
                            dve.wait_ge(s_ready, n + 1)
                            nc.vector.tensor_reduce(S_sum[:, 0, :], S[:, 0, :, :].rearrange("p j w -> p w j"), AX_X,
                                                    ALU.add).then_inc(sum_ready, 1)
                            dve.wait_ge(agg0, n + 1)
                            dve.wait_ge(acc0, n + 1)
                            accumulate(dve, ps_agg[0][:, 0:W], acc_x, W * k)
                            accumulate(dve, ps_agg[0][:, W:2 * W], acc_e, W * k)
                            accumulate(dve, ps_agg[0][0:1, 2 * W:3 * W], acc_deg, W * k).then_inc(acc0, 1)

                    nc.vector.memset(acc_x[:, :], 0.0).then_inc(acc0, 1)
                    groups(dve, step)

                @block.tensor
                def _(pe):
                    def step(g, last):
                        pe.wait_ge(gath0[0], TILES * DMA * (g + 1))
                        wait_apart(pe, edge_in[0], DMA * (g + 1 + last))
                        with pe.Fori(0, WINDOWS) as k:
                            n = WINDOWS * g + k
                            pe.wait_ge(s_ready, n + 1)
                            pe.wait_ge(acc0, n + 1)
                            for at, lhs_at in ((0, 0), (W, GE)):
                                for j in range(TILES):
                                    nc.tensor.matmul(ps_agg[0][:, at:at + W], ring[:, 0, lhs_at + j * D:lhs_at + (j + 1) * D],
                                                     S[:, 0, j, :], start=j == 0, stop=j == TILES - 1)
                            pe.wait_ge(sum_ready, n + 1)
                            nc.tensor.matmul(ps_agg[0][0:1, 2 * W:3 * W], ones[:, 0:1], S_sum[:, 0, :], start=True,
                                             stop=True).then_inc(agg0, 1)

                    groups(pe, step)

            with nc.Block() as block:
                @block.sync
                def _(sp):
                    pairs(sp, lambda sp, t: sp_x_pair(sp, t, is_last_pair(t)))

                @block.vector
                def _(dve):
                    pairs(dve, dve_sum0, dve_norm0, dve_parts0)

                @block.tensor
                def _(pe):
                    pairs(pe, lambda pe, t: pe_x0(pe, t, is_last_pair(t)), pe_products0, pe_mix0, pe_turn0, pe_pq0)

                @block.scalar
                def _(act):
                    act.wait_ge(acc0, WINDOWS * G + 1)
                    pairs(act, act_cut0, act_x0, act_products0, act_turn0, act_store0)
                    tables_stored(act)

            with nc.Block() as block:
                @block.sync
                def _(sp):
                    def step(g, last):
                        load_indices(sp, g, last, acc1, src_in1[0])
                        if last:
                            sp.dma_start(dst_slot[0:REST_P, 1, :], dst_rest).then_inc(row_in[0], DMA)
                            sp.dma_start(dst_slot[REST_P:REST_P + 1, 1, 0:REST_J], dst_end).then_inc(row_in[0], DMA)
                        else:
                            sp.dma_start(dst_slot[:, 1, :], dst_g[g]).then_inc(row_in[0], DMA)

                    sp.wait_ge(dst_in[1], DMA)
                    groups(sp, step)

                @block.gpsimd
                def _(pool):
                    def step(g, last):
                        wait_apart(pool, src_in1[0], DMA * (g + 1 + last))
                        wait_apart(pool, row_in[0], DMA * (g + 1 + last))
                        wait_apart(pool, acc1, WINDOWS * g + 1)
                        for j in range(TILES):
                            nc.gpsimd.indirect_dma_start(
                                out=ring[:, 0, 2 * j * D:2 * (j + 1) * D], out_offset=None, in_=table,
                                in_offset=bass.IndirectOffsetOnAxis(ap=src_slot[:, 0, j:j + 1], axis=0),
                            ).then_inc(gath1[0], DMA)
                            nc.gpsimd.indirect_dma_start(
                                out=q_rows[:, 3 * j * D:3 * (j + 1) * D], out_offset=None, in_=q_parts,
                                in_offset=bass.IndirectOffsetOnAxis(ap=dst_slot[:, 1, j:j + 1], axis=0),
                            ).then_inc(gath1[1], DMA)

                    groups(pool, step)

                @block.vector
                def _(dve):
                    def step(g, last):
                        start_windows(dve, g, last, G + 1)
                        dve_logits(dve, 0, g, 0)
                        wait_apart(dve, sig_done, g + 1)
                        with dve.Fori(0, WINDOWS) as k:
                            n = WINDOWS * g + k
                            next_window(dve, REL_STEPS * g + k + L1_REL + 1)
                            for j in range(TILES):
                                done = nc.vector.tensor_scalar(S[:, 0, j, :], iota_w[:, :], rel[:, j:j + 1],
                                                               weight[:, 0, j:j + 1], ALU.is_equal, ALU.mult)
                            done.then_inc(sw_ready, 1)
                            dve.wait_ge(agg1, n + 1)
                            dve.wait_ge(acc1, n + 1)
                            accumulate(dve, ps_agg[0][:, 0:W], acc_x, W * k).then_inc(acc1, 1)

                    nc.vector.memset(acc_x[:, :], 0.0).then_inc(acc1, 1)
                    groups(dve, step)

                @block.tensor
                def _(pe):
                    def step(g, last):
                        pe.wait_ge(gath1[0], TILES * DMA * (g + 1))
                        pe.wait_ge(gath1[1], TILES * DMA * (g + 1))
                        pe.wait_ge(acc1, WINDOWS * g + 1)
                        for j in range(TILES):
                            cols = ps4[j // 4][:, (j % 4) * D:(j % 4 + 1) * D]
                            nc.tensor.matmul(cols, ident[:, :], ring[:, 0, (2 * j + 1) * D:(2 * j + 2) * D], start=True, stop=False)
                            for k in range(3):
                                done = nc.tensor.matmul(cols, identb[:, :], q_rows[:, (3 * j + k) * D:(3 * j + k + 1) * D],
                                                        start=False, stop=k == 2)
                            if j % 4 == 3:
                                done.then_inc(h_done, 1)
                        with pe.Fori(0, WINDOWS) as k:
                            n = WINDOWS * g + k
                            pe.wait_ge(sw_ready, n + 1)
                            pe.wait_ge(acc1, n + 1)
                            for j in range(TILES):
                                done = nc.tensor.matmul(ps_agg[0][:, 0:W], ring[:, 0, 2 * j * D:(2 * j + 1) * D], S[:, 0, j, :],
                                                        start=j == 0, stop=j == TILES - 1)
                            done.then_inc(agg1, 1)

                    groups(pe, step)

                @block.scalar
                def _(act):
                    groups(act, lambda g, last: act_weights(act, 0, g))

            with nc.Block() as block:
                @block.sync
                def _(sp):
                    pairs(sp, sp_x1_pair)

                @block.vector
                def _(dve):
                    pairs(dve, dve_first1, dve_second1, dve_third1)

                @block.tensor
                def _(pe):
                    pairs(pe, pe_turn1)

                @block.scalar
                def _(act):
                    act.wait_ge(acc1, WINDOWS * G + 1)
                    pairs(act, act_cut1, lambda act, t: act_store1(act, t, is_last_pair(t)))
                    act.wait_ge(fin_out, DMA * (PAIRS + 1))

        with nc.If(fitting == G):
            windowed()
        with nc.Else():
            general()


_INS = ['x', 'src', 'dst', 'edge_attr_128', 'L0_gnn_W_msg_w', 'L0_gnn_W_msg_b', 'L0_gnn_W_app_w', 'L0_gnn_W_app_b',
        'L1_gnn_W1', 'L1_gnn_b1', 'L1_gnn_W2', 'L1_gnn_b2', 'L1_gnn_gamma', 'L1_gnn_beta']


def kernel(**inputs):
    import numpy as _np
    import concourse.bacc as _bacc
    from concourse import mybir as _mybir
    from concourse.bass_utils import run_bass_kernel_spmd as _run

    nc = _bacc.Bacc("TRN2", target_bir_lowering=False, num_devices=1)
    arrays, args = {}, []
    for name in _INS:
        a = _np.ascontiguousarray(inputs[name])
        arrays[f"in_{name}_dram"] = a
        args.append(nc.dram_tensor(f"in_{name}_dram", a.shape, _mybir.dt.from_np(a.dtype), kind="ExternalInput").ap())
    args.append(nc.dram_tensor("out_0_dram", (N, D), F32, kind="ExternalOutput").ap())
    build(nc, *args)
    r = _run(nc, [arrays], core_ids=[0])
    return r.results[0]["out_0_dram"]
```
